# Optimizing a Trainium2 kernel written in Bass

```python
import numpy as np
import jax
import jax.numpy as jnp

def _softmax(x, axis=-1):
    return jax.nn.softmax(x, axis=axis)

def _gelu(x):
    return jax.nn.gelu(x, approximate=True)

def _silu(x):
    return jax.nn.silu(x)

def _sigmoid(x):
    return jax.nn.sigmoid(x)

def _layernorm(x, axis=-1, eps=1e-05):
    m = jnp.mean(x, axis=axis, keepdims=True)
    v = jnp.var(x, axis=axis, keepdims=True)
    return (x - m) / jnp.sqrt(v + eps)

def _scatter_add(tgt, idx, src, axis=0):
    return tgt.at[idx].add(src)

def _segment_sum(src, seg, n):
    return jax.ops.segment_sum(src, seg, n)
kernel_name = 'mk_adj_resnorm_d2_adj_r2_bb3e44'

def setup_inputs(seed: int=0):
    np.random.seed(seed)
    _w = jnp.asarray

    def _rec_inputs():
        import jax
        import jax.numpy as jnp
        _gk = jax.random.key(seed)
        x = -0.0002928 + 1 * jax.random.normal(jax.random.fold_in(_gk, 1), (64, 128, 128), jnp.float32)
        _a = jax.random.bernoulli(jax.random.fold_in(_gk, 2), 0.03125, (64, 128, 128))
        _a = jnp.logical_or(_a, jnp.swapaxes(_a, -1, -2))
        _a = jnp.logical_or(_a, jnp.eye(128, dtype=bool))
        adj = _a.astype(jnp.int32)
        _nm = jnp.ones((64, 128), dtype=bool)
        nodemask = jnp.where(_nm, 1.0, 0.0).astype(jnp.float32)
        return (x, adj, nodemask)
    x, adj, nodemask = _rec_inputs()

    def _L0_gnn_setup():
        import jax, jax.numpy as jnp
        import numpy as np
        LEAKY_SLOPE = 0.2
        NEG_INF = -9000000000000000.0

        def _edge_scores(h, a_k):
            e = jnp.einsum('bid,bjd->bij', h * a_k[:, 0], h)
            return jax.nn.leaky_relu(e, negative_slope=LEAKY_SLOPE)
        key = jax.random.key(seed)
        k1, k2, k3, k4, k5, k6 = jax.random.split(key, 6)
        B, N, D = (32, 256, 128)
        hidden = jax.random.normal(k1, (B, N, D), dtype=jnp.float32)
        adj = jax.random.randint(k2, (B, N, N), 0, 5, dtype=jnp.int32)
        a_0 = jax.random.normal(k3, (D, 1), dtype=jnp.float32)
        a_1 = jax.random.normal(k4, (D, 1), dtype=jnp.float32)
        a_2 = jax.random.normal(k5, (D, 1), dtype=jnp.float32)
        a_3 = jax.random.normal(k6, (D, 1), dtype=jnp.float32)
        return {'hidden': hidden, 'adj': adj, 'a_0': a_0, 'a_1': a_1, 'a_2': a_2, 'a_3': a_3}
    _L0_gnn_all = _L0_gnn_setup()
    _L0_gnn_in = {k: v for k, v in _L0_gnn_all.items() if k in ('a_0', 'a_1', 'a_2', 'a_3')}
    del _L0_gnn_all

    def _L1_gnn_setup():
        import jax, jax.numpy as jnp
        import numpy as np
        D_MODEL = 128
        NUM_REL = 40

        def _direction(x, W, Wg, b, bg, adj, rel_ids):
            h = x @ W.T
            g = h @ Wg.T
            vals = (h[:, :, None, :] + b) * jax.nn.sigmoid(g[:, :, None, :] + bg)
            onehot = (adj[..., None] == rel_ids).astype(h.dtype)
            return jnp.einsum('bnmr,bmrd->bnd', onehot, vals)
        key = jax.random.key(seed)
        ks = jax.random.split(key, 16)
        B, N, d = (2, 256, D_MODEL)
        s = 0.02
        inp = {'node': jax.random.normal(ks[0], (B, N, d), dtype=jnp.float32), 'node_mask': jnp.ones((B, N), dtype=jnp.float32), 'adj_mat': jax.random.randint(ks[1], (B, N, N), 0, 41, dtype=jnp.int32), 'W_fwd': jax.random.normal(ks[2], (d, d), dtype=jnp.float32) * s, 'W_bwd': jax.random.normal(ks[3], (d, d), dtype=jnp.float32) * s, 'W_loop': jax.random.normal(ks[4], (d, d), dtype=jnp.float32) * s, 'Wg_fwd': jax.random.normal(ks[5], (d, d), dtype=jnp.float32) * s, 'Wg_bwd': jax.random.normal(ks[6], (d, d), dtype=jnp.float32) * s, 'Wg_loop': jax.random.normal(ks[7], (d, d), dtype=jnp.float32) * s, 'b_fwd': jax.random.normal(ks[8], (NUM_REL - 1, d), dtype=jnp.float32) * s, 'b_bwd': jax.random.normal(ks[9], (NUM_REL - 1, d), dtype=jnp.float32) * s, 'b_loop': jax.random.normal(ks[10], (1, d), dtype=jnp.float32) * s, 'bg_fwd': jax.random.normal(ks[11], (NUM_REL - 1, d), dtype=jnp.float32) * s, 'bg_bwd': jax.random.normal(ks[12], (NUM_REL - 1, d), dtype=jnp.float32) * s, 'bg_loop': jax.random.normal(ks[13], (1, d), dtype=jnp.float32) * s}
        return inp
    _L1_gnn_all = _L1_gnn_setup()
    _L1_gnn_in = {k: v for k, v in _L1_gnn_all.items() if k in ('W_fwd', 'W_bwd', 'W_loop', 'Wg_fwd', 'Wg_bwd', 'Wg_loop', 'b_fwd', 'b_bwd', 'b_loop', 'bg_fwd', 'bg_bwd', 'bg_loop')}
    del _L1_gnn_all
    return {'x': x, 'adj': adj, 'nodemask': nodemask, 'L0_gnn_a_0': _L0_gnn_in['a_0'], 'L0_gnn_a_1': _L0_gnn_in['a_1'], 'L0_gnn_a_2': _L0_gnn_in['a_2'], 'L0_gnn_a_3': _L0_gnn_in['a_3'], 'L1_gnn_W_fwd': _L1_gnn_in['W_fwd'], 'L1_gnn_W_bwd': _L1_gnn_in['W_bwd'], 'L1_gnn_W_loop': _L1_gnn_in['W_loop'], 'L1_gnn_Wg_fwd': _L1_gnn_in['Wg_fwd'], 'L1_gnn_Wg_bwd': _L1_gnn_in['Wg_bwd'], 'L1_gnn_Wg_loop': _L1_gnn_in['Wg_loop'], 'L1_gnn_b_fwd': _L1_gnn_in['b_fwd'], 'L1_gnn_b_bwd': _L1_gnn_in['b_bwd'], 'L1_gnn_b_loop': _L1_gnn_in['b_loop'], 'L1_gnn_bg_fwd': _L1_gnn_in['bg_fwd'], 'L1_gnn_bg_bwd': _L1_gnn_in['bg_bwd'], 'L1_gnn_bg_loop': _L1_gnn_in['bg_loop']}

def reference(x, adj, nodemask, L0_gnn_a_0, L0_gnn_a_1, L0_gnn_a_2, L0_gnn_a_3, L1_gnn_W_fwd, L1_gnn_W_bwd, L1_gnn_W_loop, L1_gnn_Wg_fwd, L1_gnn_Wg_bwd, L1_gnn_Wg_loop, L1_gnn_b_fwd, L1_gnn_b_bwd, L1_gnn_b_loop, L1_gnn_bg_fwd, L1_gnn_bg_bwd, L1_gnn_bg_loop):
    import jax
    import jax.numpy as jnp

    def _L0_gnn_ref(hidden, adj, a_0, a_1, a_2, a_3):
        import jax, jax.numpy as jnp
        import numpy as np
        LEAKY_SLOPE = 0.2
        NEG_INF = -9000000000000000.0

        def _edge_scores(h, a_k):
            e = jnp.einsum('bid,bjd->bij', h * a_k[:, 0], h)
            return jax.nn.leaky_relu(e, negative_slope=LEAKY_SLOPE)
        h = hidden
        e_0 = _edge_scores(h, a_0)
        e_1 = _edge_scores(h, a_1)
        e_2 = _edge_scores(h, a_2)
        e_3 = _edge_scores(h, a_3)
        scores = jnp.where(adj == 1, e_0, NEG_INF)
        scores = jnp.where(adj == 2, e_1, scores)
        scores = jnp.where(adj == 3, e_2, scores)
        scores = jnp.where(adj == 4, e_3, scores)
        alpha = jax.nn.softmax(scores, axis=-1)
        return jnp.einsum('bij,bjd->bid', alpha, h)

    def _L1_gnn_ref(node, node_mask, adj_mat, W_fwd, W_bwd, W_loop, Wg_fwd, Wg_bwd, Wg_loop, b_fwd, b_bwd, b_loop, bg_fwd, bg_bwd, bg_loop):
        import jax, jax.numpy as jnp
        import numpy as np
        D_MODEL = 128
        NUM_REL = 40

        def _direction(x, W, Wg, b, bg, adj, rel_ids):
            h = x @ W.T
            g = h @ Wg.T
            vals = (h[:, :, None, :] + b) * jax.nn.sigmoid(g[:, :, None, :] + bg)
            onehot = (adj[..., None] == rel_ids).astype(h.dtype)
            return jnp.einsum('bnmr,bmrd->bnd', onehot, vals)
        rels = jnp.arange(2, NUM_REL + 1, dtype=adj_mat.dtype)
        rel1 = jnp.array([1], dtype=adj_mat.dtype)
        adj_t = jnp.swapaxes(adj_mat, -1, -2)
        out = _direction(node, W_fwd, Wg_fwd, b_fwd, bg_fwd, adj_mat, rels)
        out = out + _direction(node, W_bwd, Wg_bwd, b_bwd, bg_bwd, adj_t, rels)
        out = out + _direction(node, W_loop, Wg_loop, b_loop, bg_loop, adj_t, rel1)
        return jax.nn.relu(out)
    x = _layernorm(x + _L0_gnn_ref(x, adj, L0_gnn_a_0, L0_gnn_a_1, L0_gnn_a_2, L0_gnn_a_3), axis=-1)
    x = _layernorm(x + _L1_gnn_ref(x, nodemask, adj, L1_gnn_W_fwd, L1_gnn_W_bwd, L1_gnn_W_loop, L1_gnn_Wg_fwd, L1_gnn_Wg_bwd, L1_gnn_Wg_loop, L1_gnn_b_fwd, L1_gnn_b_bwd, L1_gnn_b_loop, L1_gnn_bg_fwd, L1_gnn_bg_bwd, L1_gnn_bg_loop), axis=-1)
    return x

_drawn_inputs = setup_inputs


def setup_inputs(seed=0):
    import zlib

    import numpy as np

    out = dict(_drawn_inputs(seed))
    spreads = {}
    factors = {'L1_gnn_Wg_loop': 8.0, 'L1_gnn_bg_loop': 22.462}
    for name, (base, spread) in spreads.items():
        noise = np.random.default_rng([zlib.crc32(name.encode()), seed]).standard_normal(out[name].shape)
        drawn = base * np.exp(spread * noise) if base else spread * noise
        out[name] = jnp.asarray(drawn.astype(out[name].dtype))
    for name, factor in factors.items():
        out[name] = (out[name] * factor).astype(out[name].dtype)
    return out
```

```python
from contextlib import ExitStack

import concourse.bass as bass
from concourse import mybir

ALU = mybir.AluOpType
ACT = mybir.ActivationFunctionType
F32 = mybir.dt.float32
BF16 = mybir.dt.bfloat16
I32 = mybir.dt.int32
AX_X = mybir.AxisListType.X

P = 128
G = 4
W = G * P
SLOPE = 0.2
EPS = 1e-5
PENALTY = 2.0 ** 120
NEG_INF = -9000000000000000.0
KINDS = 4
RELATIONS = 40
LOOP, FWD, BWD = range(3)
FLOAT_MAX = 3.0e38

LAG_ATTEND = 1
LAG_GATE = 2
LAG_SUM = 3
UNROLL = 4


def program(nc, x, adj, a_0, a_all, w, wg_t, b_loop, bg_loop, b_fwd, bg_fwd, b_bwd, bg_bwd, out):
    n_groups = x.shape[0] // G
    x_v = x.rearrange("(k g) n d -> k n g d", g=G)
    adj_v = adj.rearrange("(k g) n d -> k n g d", g=G)
    out_v = out.rearrange("(k g) n d -> k n g d", g=G)

    with ExitStack() as ctx:
        def sb(name, shape, dt=F32):
            return ctx.enter_context(nc.sbuf_tensor(name, shape, dt))

        def ps(name, shape, dt=F32):
            return ctx.enter_context(nc.psum_tensor(name, shape, dt))

        def sem(name):
            return ctx.enter_context(nc.semaphore(name))

        ident = sb("ident", [P, P])
        ident_bf = sb("ident_bf", [P, P], BF16)
        ones3 = sb("ones3", [3, P], BF16)
        ones_col = sb("ones_col", [P, 1])
        minus_half = sb("minus_half", [P, G])
        a_col = sb("a_col", [P, 1])
        w_rows = sb("w_rows", [P, 3, P])
        w_mid = sb("w_mid", [P, P])
        wg_s = sb("wg_s", [P, 3, P])
        w_both = sb("w_both", [P, 2 * P])
        w_stats = sb("w_stats", [P, 6])
        w_mean = sb("w_mean", [P, 2])
        b_rows = sb("b_rows", [3, 2 * P])
        b_rest = sb("b_rest", [3, 2, 2 * P])
        b_part = sb("b_part", [3, 3, 2 * P], BF16)
        b_sum = sb("b_sum", [3, 2, 2 * P], BF16)
        b_parts = sb("b_parts", [3, 2, 2 * P], BF16)

        x_s = sb("x_s", [P, 4, G, P])
        adj_s = sb("adj_s", [P, 4, G, P], I32)
        mask = sb("mask", [P, 4, G, P])
        beyond = sb("beyond", [P, 2, G, P], BF16)
        above = sb("above", [P, n_groups])
        above_all = sb("above_all", [P, 1])
        general = sb("general", [1, 1], I32)
        pen = sb("pen", [P, 2, G, P], BF16)
        xt = sb("xt", [P, 2, G, P])
        xat = sb("xat", [P, 2, G, P])
        rel4 = sb("rel4", [P, 2, G, P])
        nscore = sb("nscore", [P, 2, G, P])
        nmax = sb("nmax", [P, 2, G])
        prob = sb("prob", [P, 2, G, P])
        psumz = sb("psumz", [P, 2, G])
        rz = sb("rz", [P, 2, G])
        prob_t = sb("prob_t", [P, 2, G, P])
        res1 = sb("res1", [P, 2, G, P])
        st1 = sb("st1", [P, 2, G, 6])
        mv1 = sb("mv1", [P, 2, G, 2])
        rs1 = sb("rs1", [P, 2, 2, G])
        y = sb("y", [P, 2, G, P])
        y_t = sb("y_t", [P, 2, G, P])
        th = sb("th", [P, 2, G, P])
        vals = sb("vals", [P, 2, G, P])
        res2 = sb("res2", [P, 2, G, P])
        st2 = sb("st2", [P, 2, G, 6])
        mv2 = sb("mv2", [P, 2, G, 2])
        rs2 = sb("rs2", [P, 2, 2, G])
        cent = sb("cent", [P, G, P])
        out_s = sb("out_s", [P, 2, G, P])

        p_xt = ps("p_xt", [P, G, P])
        p_e = ps("p_e", [P, G, P])
        p_ut = ps("p_ut", [P, G, P])
        p_o = ps("p_o", [P, G, P])
        p_yt = ps("p_yt", [P, G, P])
        p_hg = ps("p_hg", [P, G, 2, P])
        p_ag = ps("p_ag", [P, G, P])

        w_loaded = sem("w_loaded")
        x_loaded = [sem(f"x_loaded{i}") for i in range(4)]
        adj_loaded = [sem(f"adj_loaded{i}") for i in range(4)]
        stored = [sem(f"stored{i}") for i in range(2)]
        const_done = sem("const_done")
        ident_done = sem("ident_done")
        w_step = sem("w_step")
        b_step = sem("b_step")
        w_pe = sem("w_pe")
        w_ready = sem("w_ready")
        sum_done = sem("sum_done")
        general_known = sem("general_known")
        mask_done = sem("mask_done")
        above_done = sem("above_done")
        pen_done = sem("pen_done")
        tx_done = sem("tx_done")
        xt_done = sem("xt_done")
        e_done = sem("e_done")
        rel4_done = sem("rel4_done")
        score_done = sem("score_done")
        exp_done = sem("exp_done")
        tu_done = sem("tu_done")
        ut_done = sem("ut_done")
        av_done = sem("av_done")
        rz_done = sem("rz_done")
        r1_done = sem("r1_done")
        st1_done = sem("st1_done")
        mv1_done = sem("mv1_done")
        pool1 = sem("pool1")
        y_done = sem("y_done")
        ty_done = sem("ty_done")
        yt_done = sem("yt_done")
        hg_done = sem("hg_done")
        tanh_done = sem("tanh_done")
        vals_done = sem("vals_done")
        ag_done = sem("ag_done")
        r2_done = sem("r2_done")
        st2_done = sem("st2_done")
        mv2_done = sem("mv2_done")
        pool2 = sem("pool2")
        cent_done = sem("cent_done")
        out_done = sem("out_done")

        wait_over = {nc.vector: sem("dve_wait_over"), nc.gpsimd: sem("pool_wait_over"),
                     nc.sync: sem("sp_wait_over")}

        g_adj = sb("g_adj", [P, P], I32)
        g_x = sb("g_x", [P, P])
        g_a = sb("g_a", [P, KINDS])
        g_w = sb("g_w", [P, 3, 2, P])
        g_adjf = sb("g_adjf", [P, 2, P])
        g_xt = sb("g_xt", [P, P])
        g_xa = sb("g_xa", [P, KINDS, P])
        g_fifth = sb("g_fifth", [P, KINDS, P])
        g_leaky = sb("g_leaky", [P, KINDS, P])
        g_is = sb("g_is", [P, KINDS, P], I32)
        g_score = sb("g_score", [P, P])
        g_nmax = sb("g_nmax", [P, 1])
        g_prob = sb("g_prob", [P, P])
        g_z = sb("g_z", [P, 1])
        g_rz = sb("g_rz", [P, 1])
        g_prob_t = sb("g_prob_t", [P, P])
        g_res = sb("g_res", [P, P])
        g_stats = sb("g_stats", [P, 6])
        g_mv = sb("g_mv", [P, 2])
        g_var = sb("g_var", [P, 1])
        g_rstd = sb("g_rstd", [P, 1])
        g_y = sb("g_y", [P, P])
        g_y_t = sb("g_y_t", [P, P])
        g_hg = sb("g_hg", [P, 3, 2, P])
        g_rel = sb("g_rel", [P, 1])
        g_bias = sb("g_bias", [P, 2, P])
        g_sel = sb("g_sel", [P, P])
        g_h = sb("g_h", [P, P])
        g_g = sb("g_g", [P, P])
        g_tanh = sb("g_tanh", [P, P])
        g_vals = sb("g_vals", [P, P])
        g_acc = sb("g_acc", [P, P])
        g_out = sb("g_out", [P, P])

        n_graphs = x.shape[0]
        n_rel = [1, b_fwd.shape[0], b_bwd.shape[0]]
        first_rel = [1, 2, 2]
        terms = sum(n_rel)
        biases = [(b_loop, bg_loop), (b_fwd, bg_fwd), (b_bwd, bg_bwd)]

        g_a_loaded = sem("g_a_loaded")
        g_w_made = sem("g_w_made")
        g_w_ready = sem("g_w_ready")
        g_loaded = sem("g_loaded")
        g_stored = sem("g_stored")
        g_adjf_ready = sem("g_adjf_ready")
        g_turned = sem("g_turned")
        g_xt_ready = sem("g_xt_ready")
        g_xa_ready = sem("g_xa_ready")
        g_e_made = sem("g_e_made")
        g_attn = sem("g_attn")
        g_score_ready = sem("g_score_ready")
        g_prob_ready = sem("g_prob_ready")
        g_prob_turned = sem("g_prob_turned")
        g_prob_t_ready = sem("g_prob_t_ready")
        g_attended = sem("g_attended")
        g_rz_ready = sem("g_rz_ready")
        g_res_ready = sem("g_res_ready")
        g_stats_ready = sem("g_stats_ready")
        g_mv_ready = sem("g_mv_ready")
        g_var_ready = sem("g_var_ready")
        g_rstd_ready = sem("g_rstd_ready")
        g_y_ready = sem("g_y_ready")
        g_y_turned = sem("g_y_turned")
        g_y_t_ready = sem("g_y_t_ready")
        g_hg_made = sem("g_hg_made")
        g_hg_ready = sem("g_hg_ready")
        g_rel_set = sem("g_rel_set")
        g_bias_loaded = sem("g_bias_loaded")
        g_gate_in = sem("g_gate_in")
        g_tanh_ready = sem("g_tanh_ready")
        g_vals_ready = sem("g_vals_ready")
        g_term_made = sem("g_term_made")
        g_term_added = sem("g_term_added")
        g_out_ready = sem("g_out_ready")

        def each_term(eng, b, f, start=None):
            before = 0
            for direction in (LOOP, FWD, BWD):
                if start is not None:
                    start(b, direction)
                with eng.Fori(0, n_rel[direction]) as j:
                    f(b * terms + before + j, direction, j)
                before += n_rel[direction]

        def general_sync(sp):
            sp.wait_ge(general_known, 1)
            found = sp.value_load(general[0:1, 0:1], min_val=0, max_val=1)
            for k in range(2):
                sp.wait_ge(stored[k], 16 * (n_groups // 2))
            with sp.If(found > 0):
                sp.dma_start(g_a[:], a_all).then_inc(g_a_loaded, 16)
                with sp.Fori(0, n_graphs) as b:
                    sp.dma_start(g_x[:], x[b]).then_inc(g_loaded, 16)
                    sp.dma_start(g_adj[:], adj[b]).then_inc(g_loaded, 16)

                    def load_biases(n, direction, j):
                        for k, of in enumerate(biases[direction]):
                            sp.dma_start(g_bias[:, k], of[bass.ds(j, 1)].broadcast_to([P, P]))\
                                .then_inc(g_bias_loaded, 16)
                        wait_alone(nc.sync, g_term_added, n + 1)

                    each_term(sp, b, load_biases)
                    sp.wait_ge(g_out_ready, b + 1)
                    sp.dma_start(out[b], g_out[:]).then_inc(g_stored, 16)
                    wait_alone(nc.sync, g_stored, 16 * (b + 1))
            sp.nop()

        def general_pool(pool):
            pool.wait_ge(general_known, 1)
            found = pool.value_load(general[0:1, 0:1], min_val=0, max_val=1)
            with pool.If(found > 0):
                with pool.Fori(0, 2 * n_graphs) as n:
                    wait_alone(nc.gpsimd, g_mv_ready, n + 1)
                    nc.gpsimd.tensor_scalar(g_var[:], g_mv[:, 1:2], EPS, None, ALU.add).then_inc(g_var_ready, 1)
                    pool.wait_ge(g_var_ready, n + 1)
                    nc.gpsimd.tensor_tensor(g_rstd[:], g_var[:], minus_half[:, 0:1], ALU.pow)\
                        .then_inc(g_rstd_ready, 1)
            pool.nop()

        def general_scalar(act):
            act.wait_ge(general_known, 1)
            found = act.value_load(general[0:1, 0:1], min_val=0, max_val=1)
            with act.If(found > 0):
                with act.Fori(0, n_graphs) as b:
                    act.wait_ge(g_score_ready, b + 1)
                    nc.scalar.activation(g_prob[:], g_score[:], ACT.Exp, bias=g_nmax[:], accum_out=g_z[:])\
                        .then_inc(g_prob_ready, 1)

                    def tanh_of_gate(n, direction, j):
                        act.wait_ge(g_gate_in, 3 * (n + 1))
                        nc.scalar.activation(g_tanh[:], g_g[:], ACT.Tanh, scale=0.5).then_inc(g_tanh_ready, 1)

                    each_term(act, b, tanh_of_gate)
            act.nop()

        def general_vector(dve):
            dve.wait_ge(general_known, 1)
            found = dve.value_load(general[0:1, 0:1], min_val=0, max_val=1)
            with dve.If(found > 0):
                dve.wait_ge(g_w_made, 6)
                nc.vector.tensor_copy(g_w[:, LOOP], p_hg[:, 0]).then_inc(g_w_ready, 1)
                nc.vector.tensor_copy(g_w[:, FWD], p_hg[:, 1]).then_inc(g_w_ready, 1)
                nc.vector.tensor_copy(g_w[:, BWD], p_hg[:, 2]).then_inc(g_w_ready, 1)
                dve.wait_ge(g_a_loaded, 16)

                with dve.Fori(0, n_graphs) as b:
                    def stats(n):
                        dve.wait_ge(g_res_ready, n)
                        nc.vector.bn_stats(g_stats[:], g_res[:]).then_inc(g_stats_ready, 1)
                        wait_alone(nc.vector, g_stats_ready, n)
                        nc.vector.bn_aggr(g_mv[:], g_stats[:]).then_inc(g_mv_ready, 1)
                        dve.wait_ge(g_rstd_ready, n)

                    dve.wait_ge(g_loaded, 32 * (b + 1))
                    nc.vector.tensor_copy(g_adjf[:, 0], g_adj[:]).then_inc(g_adjf_ready, 1)
                    dve.wait_ge(g_turned, 2 * (b + 1))
                    nc.vector.tensor_copy(g_xt[:], p_xt[:, 0]).then_inc(g_xt_ready, 1)
                    nc.vector.tensor_copy(g_adjf[:, 1], p_xt[:, 1]).then_inc(g_xt_ready, 1)
                    dve.wait_ge(g_xt_ready, 2 * (b + 1))
                    for k in range(KINDS):
                        nc.vector.tensor_scalar(g_xa[:, k], g_xt[:], g_a[:, k:k + 1], None, ALU.mult)\
                            .then_inc(g_xa_ready, 1)
                    dve.wait_ge(g_e_made, b + 1)
                    nc.vector.tensor_scalar(g_fifth[:], p_e[:], SLOPE, None, ALU.mult).then_inc(g_attn, 1)
                    own = 2 + 2 * KINDS + 1
                    dve.wait_ge(g_attn, own * b + 1)
                    nc.vector.tensor_tensor(g_leaky[:], p_e[:], g_fifth[:], ALU.max).then_inc(g_attn, 1)
                    for k in range(KINDS):
                        nc.vector.tensor_scalar(g_is[:, k], g_adjf[:, 0], float(k + 1), None, ALU.is_equal)\
                            .then_inc(g_attn, 1)
                    nc.vector.memset(g_score[:], NEG_INF).then_inc(g_attn, 1)
                    for k in range(KINDS):
                        wait_alone(nc.vector, g_attn, own * b + 3 + KINDS + k)
                        nc.vector.copy_predicated(g_score[:], g_is[:, k], g_leaky[:, k]).then_inc(g_attn, 1)
                    dve.wait_ge(g_attn, own * (b + 1))
                    nc.vector.tensor_reduce(g_nmax[:], g_score[:], AX_X, ALU.max, negate=True)\
                        .then_inc(g_score_ready, 1)
                    dve.wait_ge(g_prob_turned, b + 1)
                    nc.vector.tensor_copy(g_prob_t[:], p_ut[:, 0]).then_inc(g_prob_t_ready, 1)
                    nc.vector.reciprocal(g_rz[:], g_z[:]).then_inc(g_rz_ready, 1)
                    dve.wait_ge(g_rz_ready, b + 1)
                    dve.wait_ge(g_attended, b + 1)
                    nc.vector.scalar_tensor_tensor(out=g_res[:], in0=p_o[:, 0], scalar=g_rz[:], in1=g_x[:],
                                                   op0=ALU.mult, op1=ALU.add).then_inc(g_res_ready, 1)
                    stats(2 * b + 1)
                    nc.vector.tensor_scalar(g_y[:], g_res[:], g_mv[:, 0:1], g_rstd[:], ALU.subtract, ALU.mult)\
                        .then_inc(g_y_ready, 1)
                    dve.wait_ge(g_y_turned, b + 1)
                    nc.vector.tensor_copy(g_y_t[:], p_yt[:, 0]).then_inc(g_y_t_ready, 1)
                    dve.wait_ge(g_hg_made, b + 1)
                    nc.vector.tensor_copy(g_hg[:], p_hg[:, 0:3]).then_inc(g_hg_ready, 1)
                    nc.vector.memset(g_acc[:], 0.0).then_inc(g_hg_ready, 1)
                    dve.wait_ge(g_hg_ready, 2 * (b + 1))

                    def set_relation(b, direction):
                        nc.vector.memset(g_rel[:], float(first_rel[direction])).then_inc(g_rel_set, 1)

                    def term(n, direction, j):
                        dve.wait_ge(g_rel_set, n + b * 3 + direction + 1)
                        nc.vector.tensor_scalar(g_sel[:], g_adjf[:, 1 if direction == FWD else 0], g_rel[:], 0.5,
                                                ALU.is_equal, ALU.mult).then_inc(g_gate_in, 1)
                        dve.wait_ge(g_bias_loaded, 32 * (n + 1))
                        nc.vector.tensor_tensor(g_h[:], g_hg[:, direction, 0], g_bias[:, 0], ALU.add)\
                            .then_inc(g_gate_in, 1)
                        nc.vector.tensor_tensor(g_g[:], g_hg[:, direction, 1], g_bias[:, 1], ALU.add)\
                            .then_inc(g_gate_in, 1)
                        dve.wait_ge(g_gate_in, 3 * (n + 1))
                        nc.vector.tensor_scalar(g_rel[:], g_rel[:], 1.0, None, ALU.add).then_inc(g_rel_set, 1)
                        dve.wait_ge(g_tanh_ready, n + 1)
                        nc.vector.scalar_tensor_tensor(out=g_vals[:], in0=g_tanh[:], scalar=1.0, in1=g_h[:],
                                                       op0=ALU.add, op1=ALU.mult).then_inc(g_vals_ready, 1)
                        dve.wait_ge(g_term_made, n + 1)
                        nc.vector.tensor_tensor(g_acc[:], p_ag[:, 0], g_acc[:], ALU.add).then_inc(g_term_added, 1)
                        dve.wait_ge(g_rel_set, n + b * 3 + direction + 2)
                        dve.wait_ge(g_term_added, n + 1)

                    each_term(dve, b, term, set_relation)
                    dve.wait_ge(g_term_added, terms * (b + 1))
                    nc.vector.scalar_tensor_tensor(out=g_res[:], in0=g_acc[:], scalar=0.0, in1=g_y[:],
                                                   op0=ALU.max, op1=ALU.add).then_inc(g_res_ready, 1)
                    stats(2 * b + 2)
                    nc.vector.tensor_scalar(g_out[:], g_res[:], g_mv[:, 0:1], g_rstd[:], ALU.subtract, ALU.mult)\
                        .then_inc(g_out_ready, 1)
            dve.nop()

        def general_tensor(pe):
            pe.wait_ge(general_known, 1)
            found = pe.value_load(general[0:1, 0:1], min_val=0, max_val=1)
            with pe.If(found > 0):
                pe.wait_ge(mv2_done, G * n_groups)
                for k in range(3):
                    nc.tensor.transpose(p_hg[:, k, 0], w_rows[:, k], ident[:]).then_inc(g_w_made, 1)
                    nc.tensor.matmul(p_hg[:, k, 1], w_rows[:, k], wg_s[:, k], start=True, stop=True)\
                        .then_inc(g_w_made, 1)
                pe.wait_ge(g_w_ready, 3)

                with pe.Fori(0, n_graphs) as b:
                    pe.wait_ge(g_loaded, 32 * (b + 1))
                    nc.tensor.transpose(p_xt[:, 0], g_x[:], ident[:]).then_inc(g_turned, 1)
                    pe.wait_ge(g_adjf_ready, b + 1)
                    nc.tensor.transpose(p_xt[:, 1], g_adjf[:, 0], ident[:]).then_inc(g_turned, 1)
                    pe.wait_ge(g_xa_ready, KINDS * (b + 1))
                    for k in range(KINDS):
                        last = nc.tensor.matmul(p_e[:, k], g_xa[:, k], g_xt[:], start=True, stop=True)
                    last.then_inc(g_e_made, 1)
                    pe.wait_ge(g_prob_ready, b + 1)
                    nc.tensor.transpose(p_ut[:, 0], g_prob[:], ident[:]).then_inc(g_prob_turned, 1)
                    pe.wait_ge(g_prob_t_ready, b + 1)
                    nc.tensor.matmul(p_o[:, 0], g_prob_t[:], g_x[:], start=True, stop=True).then_inc(g_attended, 1)
                    pe.wait_ge(g_y_ready, b + 1)
                    nc.tensor.transpose(p_yt[:, 0], g_y[:], ident[:]).then_inc(g_y_turned, 1)
                    pe.wait_ge(g_y_t_ready, b + 1)
                    for k in range(3):
                        last = nc.tensor.matmul(p_hg[:, k], g_y_t[:], g_w[:, k], start=True, stop=True)
                    last.then_inc(g_hg_made, 1)

                    def sum_of_relation(n, direction, j):
                        pe.wait_ge(g_vals_ready, n + 1)
                        nc.tensor.matmul(p_ag[:, 0], g_sel[:], g_vals[:], start=True, stop=True)\
                            .then_inc(g_term_made, 1)

                    each_term(pe, b, sum_of_relation)
            pe.nop()

        block = ctx.enter_context(nc.Block())

        def wait_alone(eng, semaphore, value):
            eng.wait_ge(semaphore, value)
            eng.sem_inc(wait_over[eng], 1)

        def steps(eng, stages, peeled=None):
            lags = [lag for lag, _ in stages]
            first, last = min(lags), n_groups - 1 + max(lags)
            peeled = peeled or max(lags)
            turns = (n_groups + first - peeled) // UNROLL
            looped = peeled + turns * UNROLL

            def step(t, turn=None):
                for lag, f in stages:
                    g = t - lag
                    if turn is not None:
                        f(turn * UNROLL + g, g % UNROLL)
                    elif 0 <= g < n_groups:
                        f(g, g % UNROLL)

            for t in range(first, peeled):
                step(t)
            with eng.Fori(0, turns) as turn:
                for t in range(peeled, peeled + UNROLL):
                    step(t, turn)
            for t in range(looped, last + 1):
                step(t)

        def nth(g, s, slots, per=1):
            return (g - s) // slots + 1

        @block.sync
        def _(sp):
            sp.dma_start(w_rows[:], w.rearrange("k f d -> f k d")).then_inc(w_loaded, 16)

            def load(g, s):
                sp.dma_start(x_s[:, s], x_v[g]).then_inc(x_loaded[s], 16)
                sp.dma_start(adj_s[:, s], adj_v[g]).then_inc(adj_loaded[s], 16)

            load(0, 0)
            sp.dma_start(a_col[:], a_0).then_inc(w_loaded, 16)
            sp.dma_start(wg_s[:], wg_t.rearrange("k f e -> f k e")).then_inc(w_loaded, 16)
            for k in range(3):
                sp.dma_start(b_rows[k:k + 1, 0:P], b_loop).then_inc(w_loaded, 16)
                sp.dma_start(b_rows[k:k + 1, P:2 * P], bg_loop).then_inc(w_loaded, 16)
            for g in range(1, 4):
                load(g, g)

            def store(g, s):
                sp.wait_ge(out_done, g + 1)
                sp.dma_start(out_v[g], out_s[:, s % 2]).then_inc(stored[s % 2], 16)

            with sp.Fori(0, n_groups // UNROLL - 1) as turn:
                for s in range(UNROLL):
                    g = turn * UNROLL + s
                    sp.wait_ge(r1_done, G * (g + 1))
                    sp.wait_ge(above_done, g + 1)
                    load(g + UNROLL, s)
                    store(g, s)
            for g in range(n_groups - UNROLL, n_groups):
                store(g, g % UNROLL)
            general_sync(sp)

        @block.gpsimd
        def _(pool):
            nc.gpsimd.memset(ident[:], 0.0).then_inc(const_done, 1)
            nc.gpsimd.memset(ident_bf[:], 0.0).then_inc(const_done, 1)
            nc.gpsimd.memset(ones3[:], 1.0).then_inc(const_done, 1)
            nc.gpsimd.memset(ones_col[:], 1.0).then_inc(const_done, 1)
            nc.gpsimd.memset(minus_half[:], -0.5).then_inc(const_done, 1)
            pool.wait_ge(const_done, 2)
            for m in (ident, ident_bf):
                nc.gpsimd.affine_select(out=m[:], in_=m[:], compare_op=ALU.not_equal, fill=1.0, base=0,
                                        pattern=[[-1, P]], channel_multiplier=1).then_inc(ident_done, 1)
            pool.wait_ge(const_done, 5)

            def norm1(g, s):
                k = s % 2
                wait_alone(nc.gpsimd, mv1_done, G * (g + 1))
                nc.gpsimd.tensor_scalar(rs1[:, k, 0], mv1[:, k, :, 1], EPS, None, ALU.add).then_inc(pool1, 1)
                pool.wait_ge(pool1, 2 * g + 1)
                nc.gpsimd.tensor_tensor(rs1[:, k, 1], rs1[:, k, 0], minus_half[:], ALU.pow).then_inc(pool1, 1)
                pool.wait_ge(pool1, 2 * g + 2)
                nc.gpsimd.tensor_tensor(y[:, k], res1[:, k], rs1[:, k, 1, :, None].broadcast_to([P, G, P]),
                                        ALU.mult).then_inc(y_done, 1)

            def norm2(g, s):
                k = s % 2
                wait_alone(nc.gpsimd, mv2_done, G * (g + 1))
                nc.gpsimd.tensor_scalar(rs2[:, k, 0], mv2[:, k, :, 1], EPS, None, ALU.add).then_inc(pool2, 1)
                pool.wait_ge(out_done, g)
                nc.gpsimd.tensor_tensor(cent[:], res2[:, k], mv2[:, k, :, 0:1].broadcast_to([P, G, P]),
                                        ALU.subtract).then_inc(cent_done, 1)
                pool.wait_ge(pool2, 2 * g + 1)
                nc.gpsimd.tensor_tensor(rs2[:, k, 1], rs2[:, k, 0], minus_half[:], ALU.pow).then_inc(pool2, 1)
                pool.wait_ge(pool2, 2 * g + 2)
                pool.wait_ge(cent_done, g + 1)
                pool.wait_ge(stored[k], 16 * ((g - k) // 2))
                nc.gpsimd.tensor_tensor(out_s[:, k], cent[:], rs2[:, k, 1, :, None].broadcast_to([P, G, P]),
                                        ALU.mult).then_inc(out_done, 1)

            steps(pool, [(LAG_GATE, norm1), (LAG_SUM, norm2)], peeled=LAG_SUM + 2)
            general_pool(pool)

        @block.scalar
        def _(act):
            act.wait_ge(w_pe, 2)
            nc.scalar.activation(w_both[:, 0:P], p_xt[:, 0], ACT.Copy, scale=0.5).then_inc(w_ready, 1)
            nc.scalar.activation(w_both[:, P:2 * P], p_xt[:, 1], ACT.Copy).then_inc(w_ready, 1)

            def penalty(g, s):
                act.wait_ge(mask_done, g + 1)
                nc.scalar.activation(pen[:, s % 2], mask[:, s], ACT.Copy, bias=-PENALTY,
                                     scale=PENALTY).then_inc(pen_done, 1)

            def evac_xt(g, s):
                k = s % 2
                act.wait_ge(tx_done, g + 1)
                nc.scalar.activation(xt[:, k], p_xt[:], ACT.Copy).then_inc(xt_done, 1)
                nc.scalar.activation(xat[:, k], p_xt[:], ACT.Copy, scale=a_col[:]).then_inc(xt_done, 1)

            def rel(g, s):
                act.wait_ge(e_done, g + 1)
                nc.scalar.activation(rel4[:, s % 2], p_e[:], ACT.Relu,
                                     scale=1.0 / SLOPE - 1.0).then_inc(rel4_done, 1)

            def exps(g, s):
                k = s % 2
                for i in range(G):
                    act.wait_ge(score_done, G * g + i + 1)
                    nc.scalar.activation(prob[:, k, i], nscore[:, k, i], ACT.Exp, scale=-1.0,
                                         bias=nmax[:, k, i:i + 1],
                                         accum_out=psumz[:, k, i:i + 1]).then_inc(exp_done, 1)

            def evac_ut(g, s):
                act.wait_ge(tu_done, g + 1)
                nc.scalar.activation(prob_t[:, s % 2], p_ut[:], ACT.Copy).then_inc(ut_done, 1)

            def evac_yt(g, s):
                act.wait_ge(ty_done, g + 1)
                nc.scalar.activation(y_t[:, s % 2], p_yt[:], ACT.Copy).then_inc(yt_done, 1)

            def tanh(g, s):
                act.wait_ge(hg_done, g + 1)
                nc.scalar.activation(th[:, s % 2], p_hg[:, :, 1], ACT.Tanh, scale=0.5).then_inc(tanh_done, 1)

            def look_above(g, s):
                nc.scalar.activation(beyond[:, s % 2], adj_s[:, s], ACT.Relu, bias=-1.0,
                                     accum_out=above[:, bass.ds(g, 1)]).then_inc(above_done, 1)

            steps(act, [(LAG_SUM, tanh), (0, evac_xt), (LAG_ATTEND, evac_ut), (0, rel),
                        (LAG_GATE, evac_yt), (0, exps), (-1, penalty), (-1, look_above)])
            general_scalar(act)

        @block.vector
        def _(dve):
            dve.wait_ge(w_loaded, 16 * 9)
            nc.vector.bn_stats(w_stats[:], w_rows[:, LOOP]).then_inc(w_step, 1)
            dve.wait_ge(w_step, 1)
            nc.vector.bn_aggr(w_mean[:], w_stats[:]).then_inc(w_step, 1)
            dve.wait_ge(w_step, 2)
            nc.vector.tensor_scalar(w_mid[:], w_rows[:, LOOP], w_mean[:, 0:1], None, ALU.subtract).then_inc(w_step, 1)
            nc.vector.tensor_scalar(b_rest[:, 0, 0:P], b_rows[:, 0:P], 0.5, None, ALU.mult).then_inc(b_step, 1)
            nc.vector.tensor_copy(b_rest[:, 0, P:2 * P], b_rows[:, P:2 * P]).then_inc(b_step, 1)
            dve.wait_ge(b_step, 2)
            nc.vector.tensor_copy(b_part[:, 0], b_rest[:, 0]).then_inc(b_step, 1)
            dve.wait_ge(b_step, 3)
            nc.vector.tensor_tensor(b_rest[:, 1], b_rest[:, 0], b_part[:, 0], ALU.subtract).then_inc(b_step, 1)
            dve.wait_ge(b_step, 4)
            nc.vector.tensor_copy(b_part[:, 1], b_rest[:, 1]).then_inc(b_step, 1)
            dve.wait_ge(b_step, 5)
            nc.vector.tensor_tensor(b_part[:, 2], b_rest[:, 1], b_part[:, 1], ALU.subtract).then_inc(b_step, 1)
            dve.wait_ge(ident_done, 1)
            nc.vector.tensor_scalar(b_sum[:, 0], b_part[:, 0], ident[0:3, 0:1], None, ALU.mult).then_inc(b_step, 1)
            dve.wait_ge(b_step, 7)
            nc.vector.scalar_tensor_tensor(out=b_sum[:, 1], in0=b_part[:, 1], scalar=ident[0:3, 1:2],
                                           in1=b_sum[:, 0], op0=ALU.mult, op1=ALU.add).then_inc(b_step, 1)
            dve.wait_ge(b_step, 8)
            for k in range(2):
                nc.vector.scalar_tensor_tensor(out=b_parts[:, k], in0=b_part[:, 2], scalar=ident[0:3, 2:3],
                                               in1=b_sum[:, 1], op0=ALU.mult, op1=ALU.add).then_inc(b_step, 1)

            def masks(g, s):
                dve.wait_ge(adj_loaded[s], 16 * nth(g, s, 4))
                nc.vector.tensor_scalar(mask[:, s], adj_s[:, s], 1.0, None, ALU.is_equal).then_inc(mask_done, 1)

            def scores(g, s):
                k = s % 2
                wait_alone(nc.vector, rel4_done, g + 1)
                for i in range(G):
                    nc.vector.tensor_tensor_reduce(nscore[:, k, i], p_e[:, i], rel4[:, k, i], -SLOPE, FLOAT_MAX,
                                                   ALU.add, ALU.min, nmax[:, k, i:i + 1]).then_inc(score_done, 1)

            def residual1(g, s):
                k = s % 2
                dve.wait_ge(exp_done, G * (g + 1))
                nc.vector.reciprocal(rz[:, k], psumz[:, k]).then_inc(rz_done, 1)
                dve.wait_ge(rz_done, g + 1)
                dve.wait_ge(av_done, g + 1)
                for i in range(G):
                    nc.vector.scalar_tensor_tensor(out=res1[:, k, i], in0=p_o[:, i], scalar=rz[:, k, i:i + 1],
                                                   in1=x_s[:, s, i], op0=ALU.mult, op1=ALU.add).then_inc(r1_done, 1)
                for i in range(G):
                    dve.wait_ge(r1_done, G * g + i + 1)
                    nc.vector.bn_stats(st1[:, k, i], res1[:, k, i]).then_inc(st1_done, 1)
                wait_alone(nc.vector, st1_done, G * (g + 1))
                for i in range(G):
                    nc.vector.bn_aggr(mv1[:, k, i], st1[:, k, i]).then_inc(mv1_done, 1)

            def values(g, s):
                k = s % 2
                dve.wait_ge(tanh_done, g + 1)
                nc.vector.scalar_tensor_tensor(out=vals[:, k], in0=th[:, k], scalar=1.0, in1=p_hg[:, :, 0],
                                               op0=ALU.add, op1=ALU.mult).then_inc(vals_done, 1)

            def residual2(g, s):
                k = s % 2
                dve.wait_ge(ag_done, g + 1)
                for i in range(G):
                    nc.vector.scalar_tensor_tensor(out=res2[:, k, i], in0=p_ag[:, i], scalar=0.0, in1=y[:, k, i],
                                               op0=ALU.max, op1=ALU.add).then_inc(r2_done, 1)
                for i in range(G):
                    dve.wait_ge(r2_done, G * g + i + 1)
                    nc.vector.bn_stats(st2[:, k, i], res2[:, k, i]).then_inc(st2_done, 1)
                wait_alone(nc.vector, st2_done, G * (g + 1))
                for i in range(G):
                    nc.vector.bn_aggr(mv2[:, k, i], st2[:, k, i]).then_inc(mv2_done, 1)

            steps(dve, [(LAG_SUM, values), (LAG_SUM, residual2), (-1, masks), (0, scores),
                        (LAG_ATTEND, residual1)])

            dve.wait_ge(above_done, n_groups)
            nc.vector.tensor_reduce(above_all[:], above[:], AX_X, ALU.add).then_inc(sum_done, 1)
            dve.wait_ge(sum_done, 2)
            nc.vector.tensor_scalar(general[:], p_xt[0:1, 0, 0:1], 0.0, None, ALU.is_gt).then_inc(general_known, 1)
            general_vector(dve)

        @block.tensor
        def _(pe):
            pe.wait_ge(w_step, 3)
            pe.wait_ge(ident_done, 2)
            nc.tensor.transpose(p_xt[:, 0], w_mid[:], ident[:]).then_inc(w_pe, 1)
            nc.tensor.matmul(p_xt[:, 1], w_mid[:], wg_s[:, LOOP], start=True, stop=True).then_inc(w_pe, 1)
            pe.wait_ge(w_ready, 2)
            pe.wait_ge(b_step, 10)

            def transpose_x(g, s):
                pe.wait_ge(x_loaded[s], 16 * nth(g, s, 4))
                pe.wait_ge(xt_done, 2 * g)
                for i in range(G):
                    last = nc.tensor.transpose(p_xt[:, i], x_s[:, s, i], ident[:])
                last.then_inc(tx_done, 1)

            def score(g, s):
                k = s % 2
                pe.wait_ge(pen_done, g + 1)
                nc.tensor.matmul(p_e[:], ident_bf[:], pen[:, k], start=True, stop=False, skip_group_check=True)
                pe.wait_ge(xt_done, 2 * g + 2)
                for i in range(G):
                    last = nc.tensor.matmul(p_e[:, i], xat[:, k, i], xt[:, k, i], start=False, stop=(i == G - 1),
                                            skip_group_check=True)
                last.then_inc(e_done, 1)

            def transpose_u(g, s):
                k = s % 2
                for i in range(G):
                    pe.wait_ge(exp_done, G * g + i + 1)
                    last = nc.tensor.transpose(p_ut[:, i], prob[:, k, i], ident[:])
                last.then_inc(tu_done, 1)

            def attend(g, s):
                k = s % 2
                pe.wait_ge(ut_done, g + 1)
                pe.wait_ge(r1_done, G * g)
                for i in range(G):
                    last = nc.tensor.matmul(p_o[:, i], prob_t[:, k, i], x_s[:, s, i], start=True, stop=True)
                last.then_inc(av_done, 1)

            def transpose_y(g, s):
                k = s % 2
                pe.wait_ge(y_done, g + 1)
                for i in range(G):
                    last = nc.tensor.transpose(p_yt[:, i], y[:, k, i], ident[:])
                last.then_inc(ty_done, 1)

            def gate(g, s):
                k = s % 2
                pe.wait_ge(yt_done, g + 1)
                for i in range(G):
                    if i % 2 == 0:
                        nc.tensor.matmul(p_hg[:, i:i + 2], ones3[:], b_parts[:], start=True, stop=False,
                                         skip_group_check=True)
                    last = nc.tensor.matmul(p_hg[:, i], y_t[:, k, i], w_both[:], start=False, stop=(i % 2 == 1),
                                            skip_group_check=True)
                last.then_inc(hg_done, 1)

            def neighbours(g, s):
                k = s % 2
                pe.wait_ge(vals_done, g + 1)
                for i in range(G):
                    last = nc.tensor.matmul(p_ag[:, i], mask[:, s, i], vals[:, k, i], start=True, stop=True)
                last.then_inc(ag_done, 1)

            steps(pe, [(0, transpose_x), (LAG_ATTEND, transpose_u), (LAG_SUM, neighbours), (0, score),
                       (LAG_GATE, transpose_y), (LAG_ATTEND, attend), (LAG_GATE, gate)])

            pe.wait_ge(sum_done, 1)
            nc.tensor.matmul(p_xt[0:1, 0, 0:1], above_all[:], ones_col[:], start=True, stop=True)\
                .then_inc(sum_done, 1)
            general_tensor(pe)


def kernel(x, adj, nodemask, L0_gnn_a_0, L0_gnn_a_1, L0_gnn_a_2, L0_gnn_a_3,
           L1_gnn_W_fwd, L1_gnn_W_bwd, L1_gnn_W_loop, L1_gnn_Wg_fwd, L1_gnn_Wg_bwd, L1_gnn_Wg_loop,
           L1_gnn_b_fwd, L1_gnn_b_bwd, L1_gnn_b_loop, L1_gnn_bg_fwd, L1_gnn_bg_bwd, L1_gnn_bg_loop):
    import numpy as np
    import concourse.bacc as bacc
    from concourse.bass_utils import run_bass_kernel_spmd

    def turned(a):
        return np.asarray(a).T

    arrays = {
        "x": x, "adj": adj, "a_0": L0_gnn_a_0,
        "a_all": np.concatenate([L0_gnn_a_0, L0_gnn_a_1, L0_gnn_a_2, L0_gnn_a_3], axis=1),
        "w": np.stack([L1_gnn_W_loop, L1_gnn_W_fwd, L1_gnn_W_bwd]),
        "wg_t": np.stack([turned(L1_gnn_Wg_loop), turned(L1_gnn_Wg_fwd), turned(L1_gnn_Wg_bwd)]),
        "b_loop": L1_gnn_b_loop, "bg_loop": L1_gnn_bg_loop, "b_fwd": L1_gnn_b_fwd, "bg_fwd": L1_gnn_bg_fwd,
        "b_bwd": L1_gnn_b_bwd, "bg_bwd": L1_gnn_bg_bwd,
    }
    arrays = {name: np.ascontiguousarray(a) for name, a in arrays.items()}
    nc = bacc.Bacc("TRN2", target_bir_lowering=False, num_devices=1)
    aps = {name: nc.dram_tensor(name, a.shape, mybir.dt.from_np(a.dtype), kind="ExternalInput").ap()
           for name, a in arrays.items()}
    out = nc.dram_tensor("out", arrays["x"].shape, F32, kind="ExternalOutput").ap()
    program(nc, **aps, out=out)
    r = run_bass_kernel_spmd(nc, [arrays], core_ids=[0])
    return r.results[0]["out"]
```

```python
from contextlib import ExitStack

import concourse.bass as bass
from concourse import mybir

ALU = mybir.AluOpType
ACT = mybir.ActivationFunctionType
F32 = mybir.dt.float32
BF16 = mybir.dt.bfloat16
I32 = mybir.dt.int32
AX_X = mybir.AxisListType.X
AX_XY = mybir.AxisListType.XY

P = 128
G = 4
W = G * P
SLOPE = 0.2
EPS = 1e-5
PENALTY = 2.0 ** 120
NEG_INF = -9000000000000000.0
KINDS = 4
RELATIONS = 40
LOOP, FWD, BWD = range(3)
FLOAT_MAX = 3.0e38

LAG_ATTEND = 1
LAG_GATE = 2
LAG_SUM = 3
UNROLL = 4


def program(nc, x, adj, a_0, a_all, w, wg_t, b_loop, bg_loop, b_fwd, bg_fwd, b_bwd, bg_bwd, out):
    n_groups = x.shape[0] // G
    x_v = x.rearrange("(k g) n d -> k n g d", g=G)
    adj_v = adj.rearrange("(k g) n d -> k n g d", g=G)
    out_v = out.rearrange("(k g) n d -> k n g d", g=G)

    with ExitStack() as ctx:
        def sb(name, shape, dt=F32):
            return ctx.enter_context(nc.sbuf_tensor(name, shape, dt))

        def ps(name, shape, dt=F32):
            return ctx.enter_context(nc.psum_tensor(name, shape, dt))

        def sem(name):
            return ctx.enter_context(nc.semaphore(name))

        ident = sb("ident", [P, P])
        penalties = sb("penalties", [P, P], BF16)
        ones3 = sb("ones3", [3, P], BF16)
        ones_col = sb("ones_col", [P, 1])
        minus_half = sb("minus_half", [P, G])
        a_col = sb("a_col", [P, 1])
        w_rows = sb("w_rows", [P, 3, P])
        w_mid = sb("w_mid", [P, P])
        wg_s = sb("wg_s", [P, 3, P])
        w_both = sb("w_both", [P, 2 * P])
        w_stats = sb("w_stats", [P, 6])
        w_mean = sb("w_mean", [P, 2])
        b_rows = sb("b_rows", [3, 2 * P])
        b_rest = sb("b_rest", [3, 2, 2 * P])
        b_part = sb("b_part", [3, 3, 2 * P], BF16)
        b_sum = sb("b_sum", [3, 2, 2 * P], BF16)
        b_parts = sb("b_parts", [3, 2, 2 * P], BF16)

        x_s = sb("x_s", [P, 4, G, P])
        adj_s = sb("adj_s", [P, 4, G, P], I32)
        mask = sb("mask", [P, 4, G, P])
        absent = sb("absent", [P, 2, G, P], BF16)
        sums = sb("sums", [P, 2, n_groups])
        sum_rows = sb("sum_rows", [P, 1])
        general = sb("general", [1, 1], I32)
        xt = sb("xt", [P, 2, G, P])
        xat = sb("xat", [P, 2, G, P])
        rel4 = sb("rel4", [P, 2, G, P])
        nscore = sb("nscore", [P, 2, G, P])
        nmax = sb("nmax", [P, 2, G])
        prob = sb("prob", [P, 2, G, P])
        psumz = sb("psumz", [P, 2, G])
        rz = sb("rz", [P, 2, G])
        prob_t = sb("prob_t", [P, 2, G, P])
        res1 = sb("res1", [P, 2, G, P])
        st1 = sb("st1", [P, 2, G, 6])
        mv1 = sb("mv1", [P, 2, G, 2])
        rs1 = sb("rs1", [P, 2, 2, G])
        y = sb("y", [P, 2, G, P])
        y_t = sb("y_t", [P, 2, G, P])
        th = sb("th", [P, 2, G, P])
        vals = sb("vals", [P, 2, G, P])
        res2 = sb("res2", [P, 2, G, P])
        st2 = sb("st2", [P, 2, G, 6])
        mv2 = sb("mv2", [P, 2, G, 2])
        rs2 = sb("rs2", [P, 2, 2, G])
        cent = sb("cent", [P, G, P])
        out_s = sb("out_s", [P, 2, G, P])

        p_xt = ps("p_xt", [P, G, P])
        p_e = ps("p_e", [P, G, P])
        p_ut = ps("p_ut", [P, G, P])
        p_o = ps("p_o", [P, G, P])
        p_yt = ps("p_yt", [P, G, P])
        p_hg = ps("p_hg", [P, G, 2, P])
        p_ag = ps("p_ag", [P, G, P])

        w_loaded = sem("w_loaded")
        a_loaded = sem("a_loaded")
        x_loaded = [sem(f"x_loaded{i}") for i in range(4)]
        adj_loaded = [sem(f"adj_loaded{i}") for i in range(4)]
        stored = [sem(f"stored{i}") for i in range(2)]
        const_done = sem("const_done")
        ident_done = sem("ident_done")
        w_step = sem("w_step")
        b_step = sem("b_step")
        w_pe = sem("w_pe")
        w_ready = sem("w_ready")
        sum_done = sem("sum_done")
        general_known = sem("general_known")
        mask_done = sem("mask_done")
        absent_done = sem("absent_done")
        tx_done = sem("tx_done")
        xt_done = sem("xt_done")
        e_done = sem("e_done")
        rel4_done = sem("rel4_done")
        score_done = sem("score_done")
        exp_done = sem("exp_done")
        tu_done = sem("tu_done")
        ut_done = sem("ut_done")
        av_done = sem("av_done")
        rz_done = sem("rz_done")
        r1_done = sem("r1_done")
        st1_done = sem("st1_done")
        mv1_done = sem("mv1_done")
        pool1 = sem("pool1")
        y_done = sem("y_done")
        ty_done = sem("ty_done")
        yt_done = sem("yt_done")
        hg_done = sem("hg_done")
        tanh_done = sem("tanh_done")
        vals_done = sem("vals_done")
        ag_done = sem("ag_done")
        r2_done = sem("r2_done")
        st2_done = sem("st2_done")
        mv2_done = sem("mv2_done")
        pool2 = sem("pool2")
        cent_done = sem("cent_done")
        out_done = sem("out_done")

        wait_over = {nc.vector: sem("dve_wait_over"), nc.gpsimd: sem("pool_wait_over"),
                     nc.sync: sem("sp_wait_over")}

        n_graphs = x.shape[0]
        n_rel = [1, b_fwd.shape[0], b_bwd.shape[0]]
        g_adj = sb("g_adj", [P, P], I32)
        g_x = sb("g_x", [P, P])
        g_a = sb("g_a", [P, KINDS])
        g_w = sb("g_w", [P, 3, 2, P])
        g_adjf = sb("g_adjf", [P, 2, P])
        g_xt = sb("g_xt", [P, P])
        g_xa = sb("g_xa", [P, KINDS, P])
        g_fifth = sb("g_fifth", [P, KINDS, P])
        g_leaky = sb("g_leaky", [P, KINDS, P])
        g_is = sb("g_is", [P, KINDS, P], I32)
        g_score = sb("g_score", [P, P])
        g_nmax = sb("g_nmax", [P, 1])
        g_prob = sb("g_prob", [P, P])
        g_z = sb("g_z", [P, 1])
        g_rz = sb("g_rz", [P, 1])
        g_prob_t = sb("g_prob_t", [P, P])
        g_res = sb("g_res", [P, P])
        g_stats = sb("g_stats", [P, 6])
        g_mv = sb("g_mv", [P, 2])
        g_var = sb("g_var", [P, 1])
        g_rstd = sb("g_rstd", [P, 1])
        g_y = sb("g_y", [P, P])
        g_y_t = sb("g_y_t", [P, P])
        g_hg = sb("g_hg", [P, 3, 2, P])
        g_rel = sb("g_rel", [P, 1])
        g_bias = [sb(f"g_bias{d}", [P, n, 2 * P]) for d, n in enumerate(n_rel)]
        g_sel = sb("g_sel", [P, P])
        g_h = sb("g_h", [P, P])
        g_g = sb("g_g", [P, P])
        g_tanh = sb("g_tanh", [P, P])
        g_vals = sb("g_vals", [P, P])
        g_acc = sb("g_acc", [P, P])
        g_out = sb("g_out", [P, P])

        first_rel = [1, 2, 2]
        terms = sum(n_rel)
        biases = [(b_loop, bg_loop), (b_fwd, bg_fwd), (b_bwd, bg_bwd)]

        g_a_loaded = sem("g_a_loaded")
        g_w_made = sem("g_w_made")
        g_w_ready = sem("g_w_ready")
        g_loaded = sem("g_loaded")
        g_stored = sem("g_stored")
        g_adjf_ready = sem("g_adjf_ready")
        g_turned = sem("g_turned")
        g_xt_ready = sem("g_xt_ready")
        g_xa_ready = sem("g_xa_ready")
        g_e_made = sem("g_e_made")
        g_attn = sem("g_attn")
        g_score_ready = sem("g_score_ready")
        g_prob_ready = sem("g_prob_ready")
        g_prob_turned = sem("g_prob_turned")
        g_prob_t_ready = sem("g_prob_t_ready")
        g_attended = sem("g_attended")
        g_rz_ready = sem("g_rz_ready")
        g_res_ready = sem("g_res_ready")
        g_stats_ready = sem("g_stats_ready")
        g_mv_ready = sem("g_mv_ready")
        g_var_ready = sem("g_var_ready")
        g_rstd_ready = sem("g_rstd_ready")
        g_y_ready = sem("g_y_ready")
        g_y_turned = sem("g_y_turned")
        g_y_t_ready = sem("g_y_t_ready")
        g_hg_made = sem("g_hg_made")
        g_hg_ready = sem("g_hg_ready")
        g_rel_set = sem("g_rel_set")
        g_bias_loaded = sem("g_bias_loaded")
        g_gate_in = sem("g_gate_in")
        g_tanh_ready = sem("g_tanh_ready")
        g_vals_ready = sem("g_vals_ready")
        g_term_made = sem("g_term_made")
        g_term_added = sem("g_term_added")
        g_out_ready = sem("g_out_ready")

        def each_term(eng, b, f, start=None):
            before = 0
            for direction in (LOOP, FWD, BWD):
                if start is not None:
                    start(b, direction)
                with eng.Fori(0, n_rel[direction]) as j:
                    f(b * terms + before + j, direction, j)
                before += n_rel[direction]

        def general_sync(sp):
            sp.wait_ge(general_known, 1)
            found = sp.value_load(general[0:1, 0:1], min_val=0, max_val=1)
            for k in range(2):
                sp.wait_ge(stored[k], 16 * (n_groups // 2))
            with sp.If(found > 0):
                sp.dma_start(g_a[:], a_all).then_inc(g_a_loaded, 16)
                for direction, of in enumerate(biases):
                    for k in range(2):
                        sp.dma_start(g_bias[direction][:, :, k * P:(k + 1) * P],
                                     of[k].rearrange("(a r) d -> a r d", a=1).broadcast_to([P, n_rel[direction], P]))\
                            .then_inc(g_bias_loaded, 16)
                with sp.Fori(0, n_graphs) as b:
                    sp.dma_start(g_x[:], x[b]).then_inc(g_loaded, 16)
                    sp.dma_start(g_adj[:], adj[b]).then_inc(g_loaded, 16)

                    sp.wait_ge(g_out_ready, b + 1)
                    sp.dma_start(out[b], g_out[:]).then_inc(g_stored, 16)
                    wait_alone(nc.sync, g_stored, 16 * (b + 1))
            sp.nop()

        def general_pool(pool):
            pool.wait_ge(general_known, 1)
            found = pool.value_load(general[0:1, 0:1], min_val=0, max_val=1)
            with pool.If(found > 0):
                with pool.Fori(0, 2 * n_graphs) as n:
                    wait_alone(nc.gpsimd, g_mv_ready, n + 1)
                    nc.gpsimd.tensor_scalar(g_var[:], g_mv[:, 1:2], EPS, None, ALU.add).then_inc(g_var_ready, 1)
                    pool.wait_ge(g_var_ready, n + 1)
                    nc.gpsimd.tensor_tensor(g_rstd[:], g_var[:], minus_half[:, 0:1], ALU.pow)\
                        .then_inc(g_rstd_ready, 1)
            pool.nop()

        def general_scalar(act):
            act.wait_ge(general_known, 1)
            found = act.value_load(general[0:1, 0:1], min_val=0, max_val=1)
            with act.If(found > 0):
                with act.Fori(0, n_graphs) as b:
                    act.wait_ge(g_score_ready, b + 1)
                    nc.scalar.activation(g_prob[:], g_score[:], ACT.Exp, bias=g_nmax[:], accum_out=g_z[:])\
                        .then_inc(g_prob_ready, 1)

                    def tanh_of_gate(n, direction, j):
                        act.wait_ge(g_gate_in, 3 * (n + 1))
                        nc.scalar.activation(g_tanh[:], g_g[:], ACT.Tanh, scale=0.5).then_inc(g_tanh_ready, 1)

                    each_term(act, b, tanh_of_gate)
            act.nop()

        def general_vector(dve):
            dve.wait_ge(general_known, 1)
            found = dve.value_load(general[0:1, 0:1], min_val=0, max_val=1)
            with dve.If(found > 0):
                dve.wait_ge(g_w_made, 6)
                nc.vector.tensor_copy(g_w[:, LOOP], p_hg[:, 0]).then_inc(g_w_ready, 1)
                nc.vector.tensor_copy(g_w[:, FWD], p_hg[:, 1]).then_inc(g_w_ready, 1)
                nc.vector.tensor_copy(g_w[:, BWD], p_hg[:, 2]).then_inc(g_w_ready, 1)
                dve.wait_ge(g_a_loaded, 16)
                dve.wait_ge(g_bias_loaded, 16 * 6)

                with dve.Fori(0, n_graphs) as b:
                    def stats(n):
                        dve.wait_ge(g_res_ready, n)
                        nc.vector.bn_stats(g_stats[:], g_res[:]).then_inc(g_stats_ready, 1)
                        wait_alone(nc.vector, g_stats_ready, n)
                        nc.vector.bn_aggr(g_mv[:], g_stats[:]).then_inc(g_mv_ready, 1)
                        dve.wait_ge(g_rstd_ready, n)

                    dve.wait_ge(g_loaded, 32 * (b + 1))
                    nc.vector.tensor_copy(g_adjf[:, 0], g_adj[:]).then_inc(g_adjf_ready, 1)
                    dve.wait_ge(g_turned, 2 * (b + 1))
                    nc.vector.tensor_copy(g_xt[:], p_xt[:, 0]).then_inc(g_xt_ready, 1)
                    nc.vector.tensor_copy(g_adjf[:, 1], p_xt[:, 1]).then_inc(g_xt_ready, 1)
                    dve.wait_ge(g_xt_ready, 2 * (b + 1))
                    for k in range(KINDS):
                        nc.vector.tensor_scalar(g_xa[:, k], g_xt[:], g_a[:, k:k + 1], None, ALU.mult)\
                            .then_inc(g_xa_ready, 1)
                    dve.wait_ge(g_e_made, b + 1)
                    nc.vector.tensor_scalar(g_fifth[:], p_e[:], SLOPE, None, ALU.mult).then_inc(g_attn, 1)
                    own = 2 + 2 * KINDS + 1
                    dve.wait_ge(g_attn, own * b + 1)
                    nc.vector.tensor_tensor(g_leaky[:], p_e[:], g_fifth[:], ALU.max).then_inc(g_attn, 1)
                    for k in range(KINDS):
                        nc.vector.tensor_scalar(g_is[:, k], g_adjf[:, 0], float(k + 1), None, ALU.is_equal)\
                            .then_inc(g_attn, 1)
                    nc.vector.memset(g_score[:], NEG_INF).then_inc(g_attn, 1)
                    for k in range(KINDS):
                        wait_alone(nc.vector, g_attn, own * b + 3 + KINDS + k)
                        nc.vector.copy_predicated(g_score[:], g_is[:, k], g_leaky[:, k]).then_inc(g_attn, 1)
                    dve.wait_ge(g_attn, own * (b + 1))
                    nc.vector.tensor_reduce(g_nmax[:], g_score[:], AX_X, ALU.max, negate=True)\
                        .then_inc(g_score_ready, 1)
                    dve.wait_ge(g_prob_turned, b + 1)
                    nc.vector.tensor_copy(g_prob_t[:], p_ut[:, 0]).then_inc(g_prob_t_ready, 1)
                    nc.vector.reciprocal(g_rz[:], g_z[:]).then_inc(g_rz_ready, 1)
                    dve.wait_ge(g_rz_ready, b + 1)
                    dve.wait_ge(g_attended, b + 1)
                    nc.vector.scalar_tensor_tensor(out=g_res[:], in0=p_o[:, 0], scalar=g_rz[:], in1=g_x[:],
                                                   op0=ALU.mult, op1=ALU.add).then_inc(g_res_ready, 1)
                    stats(2 * b + 1)
                    nc.vector.tensor_scalar(g_y[:], g_res[:], g_mv[:, 0:1], g_rstd[:], ALU.subtract, ALU.mult)\
                        .then_inc(g_y_ready, 1)
                    dve.wait_ge(g_y_turned, b + 1)
                    nc.vector.tensor_copy(g_y_t[:], p_yt[:, 0]).then_inc(g_y_t_ready, 1)
                    dve.wait_ge(g_hg_made, b + 1)
                    nc.vector.tensor_copy(g_hg[:], p_hg[:, 0:3]).then_inc(g_hg_ready, 1)
                    nc.vector.memset(g_acc[:], 0.0).then_inc(g_hg_ready, 1)
                    dve.wait_ge(g_hg_ready, 2 * (b + 1))

                    def set_relation(b, direction):
                        nc.vector.memset(g_rel[:], float(first_rel[direction])).then_inc(g_rel_set, 1)

                    def term(n, direction, j):
                        dve.wait_ge(g_rel_set, n + b * 3 + direction + 1)
                        nc.vector.tensor_scalar(g_sel[:], g_adjf[:, 1 if direction == FWD else 0], g_rel[:], 0.5,
                                                ALU.is_equal, ALU.mult).then_inc(g_gate_in, 1)
                        bias = g_bias[direction][:, bass.ds(j, 1)].rearrange("p a n -> p (a n)")
                        nc.vector.tensor_tensor(g_h[:], g_hg[:, direction, 0], bias[:, 0:P], ALU.add)\
                            .then_inc(g_gate_in, 1)
                        nc.vector.tensor_tensor(g_g[:], g_hg[:, direction, 1], bias[:, P:2 * P], ALU.add)\
                            .then_inc(g_gate_in, 1)
                        dve.wait_ge(g_gate_in, 3 * (n + 1))
                        nc.vector.tensor_scalar(g_rel[:], g_rel[:], 1.0, None, ALU.add).then_inc(g_rel_set, 1)
                        dve.wait_ge(g_tanh_ready, n + 1)
                        nc.vector.scalar_tensor_tensor(out=g_vals[:], in0=g_tanh[:], scalar=1.0, in1=g_h[:],
                                                       op0=ALU.add, op1=ALU.mult).then_inc(g_vals_ready, 1)
                        dve.wait_ge(g_term_made, n + 1)
                        nc.vector.tensor_tensor(g_acc[:], p_ag[:, 0], g_acc[:], ALU.add).then_inc(g_term_added, 1)
                        dve.wait_ge(g_rel_set, n + b * 3 + direction + 2)
                        dve.wait_ge(g_term_added, n + 1)

                    each_term(dve, b, term, set_relation)
                    dve.wait_ge(g_term_added, terms * (b + 1))
                    nc.vector.scalar_tensor_tensor(out=g_res[:], in0=g_acc[:], scalar=0.0, in1=g_y[:],
                                                   op0=ALU.max, op1=ALU.add).then_inc(g_res_ready, 1)
                    stats(2 * b + 2)
                    nc.vector.tensor_scalar(g_out[:], g_res[:], g_mv[:, 0:1], g_rstd[:], ALU.subtract, ALU.mult)\
                        .then_inc(g_out_ready, 1)
            dve.nop()

        def general_tensor(pe):
            pe.wait_ge(general_known, 1)
            found = pe.value_load(general[0:1, 0:1], min_val=0, max_val=1)
            with pe.If(found > 0):
                pe.wait_ge(mv2_done, G * n_groups)
                for k in range(3):
                    nc.tensor.transpose(p_hg[:, k, 0], w_rows[:, k], ident[:]).then_inc(g_w_made, 1)
                    nc.tensor.matmul(p_hg[:, k, 1], w_rows[:, k], wg_s[:, k], start=True, stop=True)\
                        .then_inc(g_w_made, 1)
                pe.wait_ge(g_w_ready, 3)

                with pe.Fori(0, n_graphs) as b:
                    pe.wait_ge(g_loaded, 32 * (b + 1))
                    nc.tensor.transpose(p_xt[:, 0], g_x[:], ident[:]).then_inc(g_turned, 1)
                    pe.wait_ge(g_adjf_ready, b + 1)
                    nc.tensor.transpose(p_xt[:, 1], g_adjf[:, 0], ident[:]).then_inc(g_turned, 1)
                    pe.wait_ge(g_xa_ready, KINDS * (b + 1))
                    for k in range(KINDS):
                        last = nc.tensor.matmul(p_e[:, k], g_xa[:, k], g_xt[:], start=True, stop=True)
                    last.then_inc(g_e_made, 1)
                    pe.wait_ge(g_prob_ready, b + 1)
                    nc.tensor.transpose(p_ut[:, 0], g_prob[:], ident[:]).then_inc(g_prob_turned, 1)
                    pe.wait_ge(g_prob_t_ready, b + 1)
                    nc.tensor.matmul(p_o[:, 0], g_prob_t[:], g_x[:], start=True, stop=True).then_inc(g_attended, 1)
                    pe.wait_ge(g_y_ready, b + 1)
                    nc.tensor.transpose(p_yt[:, 0], g_y[:], ident[:]).then_inc(g_y_turned, 1)
                    pe.wait_ge(g_y_t_ready, b + 1)
                    for k in range(3):
                        last = nc.tensor.matmul(p_hg[:, k], g_y_t[:], g_w[:, k], start=True, stop=True)
                    last.then_inc(g_hg_made, 1)

                    def sum_of_relation(n, direction, j):
                        pe.wait_ge(g_vals_ready, n + 1)
                        nc.tensor.matmul(p_ag[:, 0], g_sel[:], g_vals[:], start=True, stop=True)\
                            .then_inc(g_term_made, 1)

                    each_term(pe, b, sum_of_relation)
            pe.nop()

        block = ctx.enter_context(nc.Block())

        def wait_alone(eng, semaphore, value):
            eng.wait_ge(semaphore, value)
            eng.sem_inc(wait_over[eng], 1)

        def half(h):
            return slice(h * G // 2, (h + 1) * G // 2)

        def steps(eng, stages, peeled=None):
            lags = [lag for lag, *_ in stages]
            first, last = min(lags), n_groups - 1 + max(lags)
            peeled = peeled or max(lags)
            turns = (n_groups + first - peeled) // UNROLL
            looped = peeled + turns * UNROLL

            def step(t, turn=None):
                for lag, f, *half in stages:
                    g = t - lag
                    if turn is not None:
                        f(turn * UNROLL + g, g % UNROLL, *half)
                    elif 0 <= g < n_groups:
                        f(g, g % UNROLL, *half)

            for t in range(first, peeled):
                step(t)
            with eng.Fori(0, turns) as turn:
                for t in range(peeled, peeled + UNROLL):
                    step(t, turn)
            for t in range(looped, last + 1):
                step(t)

        def nth(g, s, slots, per=1):
            return (g - s) // slots + 1

        @block.sync
        def _(sp):
            def load(g, s):
                sp.dma_start(x_s[:, s], x_v[g]).then_inc(x_loaded[s], 16)
                sp.dma_start(adj_s[:, s], adj_v[g]).then_inc(adj_loaded[s], 16)

            sp.dma_start(a_col[:], a_0).then_inc(a_loaded, 16)
            load(0, 0)
            sp.dma_start(w_rows[:], w.rearrange("k f d -> f k d")).then_inc(w_loaded, 16)
            sp.dma_start(wg_s[:], wg_t.rearrange("k f e -> f k e")).then_inc(w_loaded, 16)
            for k in range(3):
                sp.dma_start(b_rows[k:k + 1, 0:P], b_loop).then_inc(w_loaded, 16)
                sp.dma_start(b_rows[k:k + 1, P:2 * P], bg_loop).then_inc(w_loaded, 16)
            for g in range(1, 4):
                load(g, g)

            def store(g, s):
                sp.wait_ge(out_done, g + 1)
                sp.dma_start(out_v[g], out_s[:, s % 2]).then_inc(stored[s % 2], 16)

            with sp.Fori(0, n_groups // UNROLL - 1) as turn:
                for s in range(UNROLL):
                    g = turn * UNROLL + s
                    sp.wait_ge(r1_done, G * (g + 1))
                    sp.wait_ge(mask_done, g + 1)
                    load(g + UNROLL, s)
                    store(g, s)
            for g in range(n_groups - UNROLL, n_groups):
                store(g, g % UNROLL)
            general_sync(sp)

        @block.gpsimd
        def _(pool):
            nc.gpsimd.memset(ident[:], 0.0).then_inc(const_done, 1)
            nc.gpsimd.memset(penalties[:], 0.0).then_inc(const_done, 1)
            nc.gpsimd.memset(ones3[:], 1.0).then_inc(const_done, 1)
            nc.gpsimd.memset(ones_col[:], 1.0).then_inc(const_done, 1)
            nc.gpsimd.memset(minus_half[:], -0.5).then_inc(const_done, 1)
            pool.wait_ge(const_done, 2)
            for m, fill in ((ident, 1.0), (penalties, -PENALTY)):
                nc.gpsimd.affine_select(out=m[:], in_=m[:], compare_op=ALU.not_equal, fill=fill, base=0,
                                        pattern=[[-1, P]], channel_multiplier=1).then_inc(ident_done, 1)
            pool.wait_ge(const_done, 5)

            def norm1(g, s):
                k = s % 2
                wait_alone(nc.gpsimd, mv1_done, G * (g + 1))
                nc.gpsimd.tensor_scalar(rs1[:, k, 0], mv1[:, k, :, 1], EPS, None, ALU.add).then_inc(pool1, 1)
                pool.wait_ge(pool1, 2 * g + 1)
                nc.gpsimd.tensor_tensor(rs1[:, k, 1], rs1[:, k, 0], minus_half[:], ALU.pow).then_inc(pool1, 1)
                pool.wait_ge(pool1, 2 * g + 2)
                nc.gpsimd.tensor_tensor(y[:, k], res1[:, k], rs1[:, k, 1, :, None].broadcast_to([P, G, P]),
                                        ALU.mult).then_inc(y_done, 1)

            def norm2(g, s):
                k = s % 2
                wait_alone(nc.gpsimd, mv2_done, G * (g + 1))
                nc.gpsimd.tensor_scalar(rs2[:, k, 0], mv2[:, k, :, 1], EPS, None, ALU.add).then_inc(pool2, 1)
                pool.wait_ge(out_done, g)
                nc.gpsimd.tensor_tensor(cent[:], res2[:, k], mv2[:, k, :, 0:1].broadcast_to([P, G, P]),
                                        ALU.subtract).then_inc(cent_done, 1)
                pool.wait_ge(pool2, 2 * g + 1)
                nc.gpsimd.tensor_tensor(rs2[:, k, 1], rs2[:, k, 0], minus_half[:], ALU.pow).then_inc(pool2, 1)
                pool.wait_ge(pool2, 2 * g + 2)
                pool.wait_ge(cent_done, g + 1)
                pool.wait_ge(stored[k], 16 * ((g - k) // 2))
                nc.gpsimd.tensor_tensor(out_s[:, k], cent[:], rs2[:, k, 1, :, None].broadcast_to([P, G, P]),
                                        ALU.mult).then_inc(out_done, 1)

            steps(pool, [(LAG_GATE, norm1), (LAG_SUM, norm2)], peeled=LAG_SUM + 2)
            general_pool(pool)

        @block.scalar
        def _(act):
            def masks(g, s):
                act.wait_ge(adj_loaded[s], 16 * nth(g, s, 4))
                nc.scalar.activation(absent[:, s % 2], adj_s[:, s], ACT.Relu, scale=-1.0, bias=1.0,
                                     accum_out=sums[:, 0, bass.ds(g, 1)]).then_inc(absent_done, 1)
                if not isinstance(g, int) or g >= 4:
                    act.wait_ge(ag_done, 2 * (g - 3))
                nc.scalar.activation(mask[:, s], adj_s[:, s], ACT.Relu,
                                     accum_out=sums[:, 1, bass.ds(g, 1)]).then_inc(mask_done, 1)

            def evac_xt(g, s):
                k = s % 2
                act.wait_ge(tx_done, g + 1)
                nc.scalar.activation(xt[:, k], p_xt[:], ACT.Copy).then_inc(xt_done, 1)
                nc.scalar.activation(xat[:, k], p_xt[:], ACT.Copy, scale=a_col[:]).then_inc(xt_done, 1)

            def rel(g, s):
                act.wait_ge(e_done, g + 1)
                nc.scalar.activation(rel4[:, s % 2], p_e[:], ACT.Relu,
                                     scale=1.0 / SLOPE - 1.0).then_inc(rel4_done, 1)

            def exps(g, s):
                k = s % 2
                for i in range(G):
                    act.wait_ge(score_done, G * g + i + 1)
                    nc.scalar.activation(prob[:, k, i], nscore[:, k, i], ACT.Exp, scale=-1.0,
                                         bias=nmax[:, k, i:i + 1],
                                         accum_out=psumz[:, k, i:i + 1]).then_inc(exp_done, 1)

            def evac_ut(g, s):
                if isinstance(g, int) and g == 0:
                    act.wait_ge(w_pe, 2)
                    nc.scalar.activation(w_both[:, 0:P], p_hg[:, 0, 0], ACT.Copy, scale=0.5).then_inc(w_ready, 1)
                    nc.scalar.activation(w_both[:, P:2 * P], p_hg[:, 0, 1], ACT.Copy).then_inc(w_ready, 1)
                act.wait_ge(tu_done, g + 1)
                nc.scalar.activation(prob_t[:, s % 2], p_ut[:], ACT.Copy).then_inc(ut_done, 1)

            def evac_yt(g, s):
                act.wait_ge(ty_done, g + 1)
                nc.scalar.activation(y_t[:, s % 2], p_yt[:], ACT.Copy).then_inc(yt_done, 1)

            def tanh(g, s, h):
                act.wait_ge(hg_done, 2 * g + h + 1)
                nc.scalar.activation(th[:, s % 2, half(h)], p_hg[:, half(h), 1], ACT.Tanh, scale=0.5)\
                    .then_inc(tanh_done, 1)

            act.wait_ge(a_loaded, 16)
            steps(act, [(LAG_SUM, tanh, 0), (LAG_SUM, tanh, 1), (0, evac_xt), (LAG_ATTEND, evac_ut), (0, rel), (LAG_GATE, evac_yt), (0, exps), (-1, masks)])
            general_scalar(act)

        @block.vector
        def _(dve):
            dve.wait_ge(w_loaded, 16 * 8)
            nc.vector.bn_stats(w_stats[:], w_rows[:, LOOP]).then_inc(w_step, 1)
            dve.wait_ge(w_step, 1)
            nc.vector.bn_aggr(w_mean[:], w_stats[:]).then_inc(w_step, 1)
            dve.wait_ge(w_step, 2)
            nc.vector.tensor_scalar(w_mid[:], w_rows[:, LOOP], w_mean[:, 0:1], None, ALU.subtract).then_inc(w_step, 1)
            nc.vector.tensor_scalar(b_rest[:, 0, 0:P], b_rows[:, 0:P], 0.5, None, ALU.mult).then_inc(b_step, 1)
            nc.vector.tensor_copy(b_rest[:, 0, P:2 * P], b_rows[:, P:2 * P]).then_inc(b_step, 1)
            dve.wait_ge(b_step, 2)
            nc.vector.tensor_copy(b_part[:, 0], b_rest[:, 0]).then_inc(b_step, 1)
            dve.wait_ge(b_step, 3)
            nc.vector.tensor_tensor(b_rest[:, 1], b_rest[:, 0], b_part[:, 0], ALU.subtract).then_inc(b_step, 1)
            dve.wait_ge(b_step, 4)
            nc.vector.tensor_copy(b_part[:, 1], b_rest[:, 1]).then_inc(b_step, 1)
            dve.wait_ge(b_step, 5)
            nc.vector.tensor_tensor(b_part[:, 2], b_rest[:, 1], b_part[:, 1], ALU.subtract).then_inc(b_step, 1)
            dve.wait_ge(ident_done, 1)
            nc.vector.tensor_scalar(b_sum[:, 0], b_part[:, 0], ident[0:3, 0:1], None, ALU.mult).then_inc(b_step, 1)
            dve.wait_ge(b_step, 7)
            nc.vector.scalar_tensor_tensor(out=b_sum[:, 1], in0=b_part[:, 1], scalar=ident[0:3, 1:2],
                                           in1=b_sum[:, 0], op0=ALU.mult, op1=ALU.add).then_inc(b_step, 1)
            dve.wait_ge(b_step, 8)
            for k in range(2):
                nc.vector.scalar_tensor_tensor(out=b_parts[:, k], in0=b_part[:, 2], scalar=ident[0:3, 2:3],
                                               in1=b_sum[:, 1], op0=ALU.mult, op1=ALU.add).then_inc(b_step, 1)

            def scores(g, s):
                k = s % 2
                wait_alone(nc.vector, rel4_done, g + 1)
                for i in range(G):
                    nc.vector.tensor_tensor_reduce(nscore[:, k, i], p_e[:, i], rel4[:, k, i], -SLOPE, FLOAT_MAX,
                                                   ALU.add, ALU.min, nmax[:, k, i:i + 1]).then_inc(score_done, 1)

            def residual1(g, s):
                k = s % 2
                dve.wait_ge(exp_done, G * (g + 1))
                nc.vector.reciprocal(rz[:, k], psumz[:, k]).then_inc(rz_done, 1)
                dve.wait_ge(rz_done, g + 1)
                dve.wait_ge(av_done, g + 1)
                for i in range(G):
                    nc.vector.scalar_tensor_tensor(out=res1[:, k, i], in0=p_o[:, i], scalar=rz[:, k, i:i + 1],
                                                   in1=x_s[:, s, i], op0=ALU.mult, op1=ALU.add).then_inc(r1_done, 1)

            def stats1(g, s):
                k = s % 2
                for i in range(G):
                    dve.wait_ge(r1_done, G * g + i + 1)
                    nc.vector.bn_stats(st1[:, k, i], res1[:, k, i]).then_inc(st1_done, 1)
                wait_alone(nc.vector, st1_done, G * (g + 1))
                for i in range(G):
                    nc.vector.bn_aggr(mv1[:, k, i], st1[:, k, i]).then_inc(mv1_done, 1)

            def values(g, s, h):
                k = s % 2
                dve.wait_ge(tanh_done, 2 * g + h + 1)
                nc.vector.scalar_tensor_tensor(out=vals[:, k, half(h)], in0=th[:, k, half(h)], scalar=1.0,
                                               in1=p_hg[:, half(h), 0], op0=ALU.add, op1=ALU.mult)\
                    .then_inc(vals_done, 1)

            def residual2(g, s):
                k = s % 2
                dve.wait_ge(ag_done, 2 * (g + 1))
                nc.vector.scalar_tensor_tensor(out=res2[:, k], in0=p_ag[:], scalar=0.0, in1=y[:, k],
                                               op0=ALU.max, op1=ALU.add).then_inc(r2_done, 1)

            def stats2(g, s):
                k = s % 2
                dve.wait_ge(r2_done, g + 1)
                for i in range(G):
                    nc.vector.bn_stats(st2[:, k, i], res2[:, k, i]).then_inc(st2_done, 1)
                wait_alone(nc.vector, st2_done, G * (g + 1))
                for i in range(G):
                    nc.vector.bn_aggr(mv2[:, k, i], st2[:, k, i]).then_inc(mv2_done, 1)

            steps(dve, [(LAG_SUM, values, 0), (LAG_SUM, values, 1), (LAG_SUM, residual2), (LAG_SUM, stats2), (0, scores), (LAG_ATTEND, residual1), (LAG_ATTEND, stats1)])

            dve.wait_ge(mask_done, n_groups)
            nc.vector.tensor_reduce(sum_rows[:], sums[:], AX_XY, ALU.add).then_inc(sum_done, 1)
            dve.wait_ge(sum_done, 2)
            nc.vector.tensor_scalar(general[:], p_xt[0:1, 0, 0:1], float(x.shape[0] * P * P), None, ALU.is_gt).then_inc(general_known, 1)
            general_vector(dve)

        @block.tensor
        def _(pe):
            pe.wait_ge(ident_done, 2)

            def transpose_x(g, s):
                pe.wait_ge(x_loaded[s], 16 * nth(g, s, 4))
                pe.wait_ge(xt_done, 2 * g)
                for i in range(G):
                    last = nc.tensor.transpose(p_xt[:, i], x_s[:, s, i], ident[:])
                last.then_inc(tx_done, 1)

            def score(g, s):
                k = s % 2
                pe.wait_ge(absent_done, g + 1)
                nc.tensor.matmul(p_e[:], penalties[:], absent[:, k], start=True, stop=False, skip_group_check=True)
                pe.wait_ge(xt_done, 2 * g + 2)
                for i in range(G):
                    last = nc.tensor.matmul(p_e[:, i], xat[:, k, i], xt[:, k, i], start=False, stop=(i == G - 1),
                                            skip_group_check=True)
                last.then_inc(e_done, 1)

            def transpose_u(g, s):
                k = s % 2
                if isinstance(g, int) and g == 0:
                    pe.wait_ge(w_step, 3)
                    nc.tensor.transpose(p_hg[:, 0, 0], w_mid[:], ident[:]).then_inc(w_pe, 1)
                    nc.tensor.matmul(p_hg[:, 0, 1], w_mid[:], wg_s[:, LOOP], start=True, stop=True)\
                        .then_inc(w_pe, 1)
                for i in range(G):
                    pe.wait_ge(exp_done, G * g + i + 1)
                    last = nc.tensor.transpose(p_ut[:, i], prob[:, k, i], ident[:])
                last.then_inc(tu_done, 1)

            def attend(g, s):
                k = s % 2
                pe.wait_ge(ut_done, g + 1)
                pe.wait_ge(r1_done, G * g)
                for i in range(G):
                    last = nc.tensor.matmul(p_o[:, i], prob_t[:, k, i], x_s[:, s, i], start=True, stop=True)
                last.then_inc(av_done, 1)

            def transpose_y(g, s):
                k = s % 2
                pe.wait_ge(y_done, g + 1)
                for i in range(G):
                    last = nc.tensor.transpose(p_yt[:, i], y[:, k, i], ident[:])
                last.then_inc(ty_done, 1)

            def gate(g, s, h):
                k = s % 2
                if isinstance(g, int) and g == 0 and h == 0:
                    pe.wait_ge(w_ready, 2)
                    pe.wait_ge(b_step, 10)
                pe.wait_ge(yt_done, g + 1)
                nc.tensor.matmul(p_hg[:, half(h)], ones3[:], b_parts[:], start=True, stop=False,
                                 skip_group_check=True)
                for i in range(2 * h, 2 * h + 2):
                    last = nc.tensor.matmul(p_hg[:, i], y_t[:, k, i], w_both[:], start=False, stop=(i % 2 == 1),
                                            skip_group_check=True)
                last.then_inc(hg_done, 1)

            def neighbours(g, s, h):
                k = s % 2
                pe.wait_ge(vals_done, 2 * g + h + 1)
                for i in range(2 * h, 2 * h + 2):
                    last = nc.tensor.matmul(p_ag[:, i], mask[:, s, i], vals[:, k, i], start=True, stop=True)
                last.then_inc(ag_done, 1)

            steps(pe, [(0, transpose_x), (LAG_ATTEND, transpose_u), (LAG_SUM, neighbours, 0), (LAG_SUM, neighbours, 1), (0, score), (LAG_GATE, transpose_y), (LAG_ATTEND, attend), (LAG_GATE, gate, 0), (LAG_GATE, gate, 1)])

            pe.wait_ge(sum_done, 1)
            nc.tensor.matmul(p_xt[0:1, 0, 0:1], sum_rows[:], ones_col[:], start=True, stop=True)\
                .then_inc(sum_done, 1)
            general_tensor(pe)


def kernel(x, adj, nodemask, L0_gnn_a_0, L0_gnn_a_1, L0_gnn_a_2, L0_gnn_a_3,
           L1_gnn_W_fwd, L1_gnn_W_bwd, L1_gnn_W_loop, L1_gnn_Wg_fwd, L1_gnn_Wg_bwd, L1_gnn_Wg_loop,
           L1_gnn_b_fwd, L1_gnn_b_bwd, L1_gnn_b_loop, L1_gnn_bg_fwd, L1_gnn_bg_bwd, L1_gnn_bg_loop):
    import numpy as np
    import concourse.bacc as bacc
    from concourse.bass_utils import run_bass_kernel_spmd

    def turned(a):
        return np.asarray(a).T

    arrays = {
        "x": x, "adj": adj, "a_0": L0_gnn_a_0,
        "a_all": np.concatenate([L0_gnn_a_0, L0_gnn_a_1, L0_gnn_a_2, L0_gnn_a_3], axis=1),
        "w": np.stack([L1_gnn_W_loop, L1_gnn_W_fwd, L1_gnn_W_bwd]),
        "wg_t": np.stack([turned(L1_gnn_Wg_loop), turned(L1_gnn_Wg_fwd), turned(L1_gnn_Wg_bwd)]),
        "b_loop": L1_gnn_b_loop, "bg_loop": L1_gnn_bg_loop, "b_fwd": L1_gnn_b_fwd, "bg_fwd": L1_gnn_bg_fwd,
        "b_bwd": L1_gnn_b_bwd, "bg_bwd": L1_gnn_bg_bwd,
    }
    arrays = {name: np.ascontiguousarray(a) for name, a in arrays.items()}
    nc = bacc.Bacc("TRN2", target_bir_lowering=False, num_devices=1)
    aps = {name: nc.dram_tensor(name, a.shape, mybir.dt.from_np(a.dtype), kind="ExternalInput").ap()
           for name, a in arrays.items()}
    out = nc.dram_tensor("out", arrays["x"].shape, F32, kind="ExternalOutput").ap()
    program(nc, **aps, out=out)
    r = run_bass_kernel_spmd(nc, [arrays], core_ids=[0])
    return r.results[0]["out"]
```

```python
from contextlib import ExitStack

import concourse.bass as bass
from concourse import mybir

ALU = mybir.AluOpType
ACT = mybir.ActivationFunctionType
F32 = mybir.dt.float32
BF16 = mybir.dt.bfloat16
I32 = mybir.dt.int32
AX_X = mybir.AxisListType.X
AX_XY = mybir.AxisListType.XY

P = 128
G = 4
W = G * P
SLOPE = 0.2
LATE = 4
EPS = 1e-5
PENALTY = 2.0 ** 120
NEG_INF = -9000000000000000.0
KINDS = 4
RELATIONS = 40
LOOP, FWD, BWD = range(3)
FLOAT_MAX = 3.0e38

UNROLL = 4

SCHEDULE = {
    "tensor": (3, """
        products:0 products:1 turn_probs:0 attend:0 products:2 turn_probs:1 attend:1 products:3 turn_probs:2
        turn_y:0 attend:2 gate_a:0 gate_b:0 turn_y:1 sum_a:0 sum_b:0 gate_a:1 gate_b:1
        """, """
        turn_probs:3 products:4 attend:3 turn_y:2 sum_a:1 sum_b:1 gate_b:2 gate_a:2
        """, """
        turn_probs:15 attend:15 sum_a:13 turn_y:14 sum_b:13 gate_a:14 gate_b:14 sum_a:14 turn_y:15 sum_b:14
        gate_a:15 gate_b:15 sum_a:15 sum_b:15
        """),
    "scalar": (3, """
        weigh:0 absent:0 relu:0 weigh:1 absent:1 exp:0 relu:1 turned_probs:0 weigh:2 absent:2 exp:1 relu:2
        turned_probs:1 weigh:3 absent:3 exp:2 relu:3 turned_probs:2 mask:0 turned_y:0 mask:1 tanh_a:0
        tanh_b:0 turned_y:1
        """, """
        weigh:4 exp:3 absent:4 turned_probs:3 tanh_b:1 tanh_a:1 mask:2 relu:4 turned_y:2
        """, """
        exp:15 turned_probs:15 tanh_a:13 mask:14 tanh_b:13 turned_y:14 finish:12 tanh_a:14 mask:15 tanh_b:14
        turned_y:15 finish:13 tanh_a:15 tanh_b:15 finish:14 finish:15
        """),
    "vector": (3, """
        scores:0 inverse:0 scores:1 residual1:0 stats1:0 means1:0 inverse:1 scores:2 residual1:1 stats1:1
        means1:1 inverse:2 scores:3 residual1:2 values_a:0 values_b:0 stats1:2 means1:2 inverse:3
        residual2:0 stats2:0 means2:0
        """, """
        values_b:1 values_a:1 residual1:3 scores:4 stats1:3 means1:3 residual2:1 stats2:1 inverse:4 means2:1
        """, """
        values_a:13 residual1:15 values_b:13 stats1:15 means1:15 residual2:13 stats2:13 values_a:14
        means2:13 values_b:14 residual2:14 stats2:14 values_a:15 means2:14 values_b:15 residual2:15
        stats2:15 means2:15
        """),
    "gpsimd": (2, """
        norm1:0 norm1:1 norm1:2 norm2:0 norm1:3 norm2:1 norm1:4
        """, """
        norm2:2 norm1:5
        """, """
        norm2:10 norm1:13 norm2:11 norm1:14 norm2:12 norm1:15 norm2:13 norm2:14 norm2:15
        """),
}


def program(nc, x, x_t, adj, a_0, a_all, w, wg_t, b_loop, b_fwd, b_bwd, out):
    n_groups = x.shape[0] // G
    x_v = x.rearrange("(k g) n d -> k n g d", g=G)
    x_t_v = x_t.rearrange("(k g) d n -> k d g n", g=G)
    adj_v = adj.rearrange("(k g) n d -> k n g d", g=G)
    out_v = out.rearrange("(k g) n d -> k n g d", g=G)

    with ExitStack() as ctx:
        def sb(name, shape, dt=F32):
            return ctx.enter_context(nc.sbuf_tensor(name, shape, dt))

        def ps(name, shape, dt=F32):
            return ctx.enter_context(nc.psum_tensor(name, shape, dt))

        def sem(name):
            return ctx.enter_context(nc.semaphore(name))

        warm = sb("warm", [P, P])
        ident = sb("ident", [P, P])
        penalties = sb("penalties", [P, P], BF16)
        ones3 = sb("ones3", [3, P], BF16)
        ones_col = sb("ones_col", [P, 1])
        minus_half = sb("minus_half", [P, G])
        minus_one = sb("minus_one", [P, G])
        a_col = sb("a_col", [P, 1])
        table_loader = sb("table_loader", [P, 1])
        w_rows = sb("w_rows", [P, 3, P])
        w_mid = sb("w_mid", [P, P])
        wg_s = sb("wg_s", [P, 3, P])
        w_both = sb("w_both", [P, 2 * P])
        w_stats = sb("w_stats", [P, 6])
        w_mean = sb("w_mean", [P, 2])
        b_rows = sb("b_rows", [3, 2 * P])
        b_rest = sb("b_rest", [3, 2, 2 * P])
        b_part = sb("b_part", [3, 3, 2 * P], BF16)
        b_sum = sb("b_sum", [3, 2, 2 * P], BF16)
        b_parts = sb("b_parts", [3, 2, 2 * P], BF16)

        x_s = sb("x_s", [P, 4, G, P])
        adj_s = sb("adj_s", [P, 4, G, P], I32)
        mask = sb("mask", [P, 4, G, P])
        absent = sb("absent", [P, 2, G, P], BF16)
        sums = sb("sums", [P, 2, n_groups])
        sum_rows = sb("sum_rows", [P, 1])
        general = sb("general", [1, 1], I32)
        xt = sb("xt", [P, 4, G, P])
        xat = sb("xat", [P, 2, G, P])
        rel4 = sb("rel4", [P, 2, G, P])
        nscore = sb("nscore", [P, 2, G, P])
        nmax = sb("nmax", [P, 4, G])
        prob = sb("prob", [P, 2, G, P])
        psumz = sb("psumz", [P, 4, G])
        rz = sb("rz", [P, 4, G])
        prob_t = sb("prob_t", [P, 2, G, P])
        res1 = sb("res1", [P, 2, G, P])
        st1 = sb("st1", [P, 4, G, 6])
        mv1 = sb("mv1", [P, 4, G, 2])
        rs1 = sb("rs1", [P, 2, 2, G])
        y = sb("y", [P, 4, G, P])
        y_t = sb("y_t", [P, 2, G, P])
        th = sb("th", [P, 2, G, P])
        vals = sb("vals", [P, 2, G, P])
        res2 = sb("res2", [P, 2, G, P])
        st2 = sb("st2", [P, 4, G, 6])
        mv2 = sb("mv2", [P, 4, G, 2])
        rs2 = sb("rs2", [P, 4, 2, G])
        shift = sb("shift", [P, 4, 2, G])
        cent = sb("cent", [P, G, P])
        out_s = sb("out_s", [P, 2, G, P])

        p_e = ps("p_e", [P, 2, G, P])
        p_ut = ps("p_ut", [P, G, P])
        p_o = ps("p_o", [P, G, P])
        p_yt = ps("p_yt", [P, G, P])
        p_hg = ps("p_hg", [P, G, 2, P])
        p_ag = ps("p_ag", [P, G, P])

        table_loaded = sem("table_loaded")
        warm_ready = sem("warm_ready")
        warmed = sem("warmed")
        w_loaded = sem("w_loaded")
        a_loaded = sem("a_loaded")
        b_loaded = sem("b_loaded")
        x_loaded = [sem(f"x_loaded{i}") for i in range(4)]
        adj_loaded = [sem(f"adj_loaded{i}") for i in range(4)]
        stored = [sem(f"stored{i}") for i in range(2)]
        const_done = sem("const_done")
        ident_done = sem("ident_done")
        w_step = sem("w_step")
        b_step = sem("b_step")
        w_pe = sem("w_pe")
        w_ready = sem("w_ready")
        sum_done = sem("sum_done")
        general_known = sem("general_known")
        mask_done = sem("mask_done")
        absent_done = sem("absent_done")
        xt_loaded = [sem(f"xt_loaded{i}") for i in range(4)]
        xat_done = sem("xat_done")
        e_done = sem("e_done")
        rel4_done = sem("rel4_done")
        score_done = sem("score_done")
        exp_done = sem("exp_done")
        tu_done = sem("tu_done")
        ut_done = sem("ut_done")
        av_done = sem("av_done")
        rz_done = sem("rz_done")
        r1_done = sem("r1_done")
        st1_done = sem("st1_done")
        mv1_done = sem("mv1_done")
        pool1 = sem("pool1")
        y_done = sem("y_done")
        ty_done = sem("ty_done")
        yt_done = sem("yt_done")
        hg_done = [sem(f"hg_done{h}") for h in range(2)]
        tanh_done = [sem(f"tanh_done{h}") for h in range(2)]
        vals_done = [sem(f"vals_done{h}") for h in range(2)]
        ag_done = [sem(f"ag_done{h}") for h in range(2)]
        r2_done = sem("r2_done")
        st2_done = sem("st2_done")
        mv2_done = sem("mv2_done")
        pool2 = sem("pool2")
        cent_done = sem("cent_done")
        out_done = sem("out_done")
        shift_done = sem("shift_done")
        finish_done = sem("finish_done")

        wait_over = {nc.vector: sem("dve_wait_over"), nc.gpsimd: sem("pool_wait_over"),
                     nc.sync: sem("sp_wait_over")}

        n_graphs = x.shape[0]
        n_rel = [1, b_fwd.shape[0], b_bwd.shape[0]]
        g_adj = sb("g_adj", [P, P], I32)
        g_x = sb("g_x", [P, P])
        g_a = sb("g_a", [P, KINDS])
        g_w = sb("g_w", [P, 3, 2, P])
        g_adjf = sb("g_adjf", [P, 2, P])
        g_xt = sb("g_xt", [P, P])
        g_xa = sb("g_xa", [P, KINDS, P])
        g_fifth = sb("g_fifth", [P, KINDS, P])
        g_leaky = sb("g_leaky", [P, KINDS, P])
        g_is = sb("g_is", [P, KINDS, P], I32)
        g_score = sb("g_score", [P, P])
        g_nmax = sb("g_nmax", [P, 1])
        g_prob = sb("g_prob", [P, P])
        g_z = sb("g_z", [P, 1])
        g_rz = sb("g_rz", [P, 1])
        g_prob_t = sb("g_prob_t", [P, P])
        g_res = sb("g_res", [P, P])
        g_stats = sb("g_stats", [P, 6])
        g_mv = sb("g_mv", [P, 2])
        g_var = sb("g_var", [P, 1])
        g_rstd = sb("g_rstd", [P, 1])
        g_y = sb("g_y", [P, P])
        g_y_t = sb("g_y_t", [P, P])
        g_hg = sb("g_hg", [P, 3, 2, P])
        g_rel = sb("g_rel", [P, 1])
        g_bias = [sb(f"g_bias{d}", [P, n, 2 * P]) for d, n in enumerate(n_rel)]
        g_sel = sb("g_sel", [P, P])
        g_h = sb("g_h", [P, P])
        g_g = sb("g_g", [P, P])
        g_tanh = sb("g_tanh", [P, P])
        g_vals = sb("g_vals", [P, P])
        g_acc = sb("g_acc", [P, P])
        g_out = sb("g_out", [P, P])

        first_rel = [1, 2, 2]
        terms = sum(n_rel)
        biases = [b_loop, b_fwd, b_bwd]

        g_a_loaded = sem("g_a_loaded")
        g_w_made = sem("g_w_made")
        g_w_ready = sem("g_w_ready")
        g_loaded = sem("g_loaded")
        g_stored = sem("g_stored")
        g_adjf_ready = sem("g_adjf_ready")
        g_turned = sem("g_turned")
        g_xt_ready = sem("g_xt_ready")
        g_xa_ready = sem("g_xa_ready")
        g_e_made = sem("g_e_made")
        g_attn = sem("g_attn")
        g_score_ready = sem("g_score_ready")
        g_prob_ready = sem("g_prob_ready")
        g_prob_turned = sem("g_prob_turned")
        g_prob_t_ready = sem("g_prob_t_ready")
        g_attended = sem("g_attended")
        g_rz_ready = sem("g_rz_ready")
        g_res_ready = sem("g_res_ready")
        g_stats_ready = sem("g_stats_ready")
        g_mv_ready = sem("g_mv_ready")
        g_var_ready = sem("g_var_ready")
        g_rstd_ready = sem("g_rstd_ready")
        g_y_ready = sem("g_y_ready")
        g_y_turned = sem("g_y_turned")
        g_y_t_ready = sem("g_y_t_ready")
        g_hg_made = sem("g_hg_made")
        g_hg_ready = sem("g_hg_ready")
        g_rel_set = sem("g_rel_set")
        g_bias_loaded = sem("g_bias_loaded")
        g_gate_in = sem("g_gate_in")
        g_tanh_ready = sem("g_tanh_ready")
        g_vals_ready = sem("g_vals_ready")
        g_term_made = sem("g_term_made")
        g_term_added = sem("g_term_added")
        g_out_ready = sem("g_out_ready")

        def each_term(eng, b, f, start=None):
            before = 0
            for direction in (LOOP, FWD, BWD):
                if start is not None:
                    start(b, direction)
                with eng.Fori(0, n_rel[direction]) as j:
                    f(b * terms + before + j, direction, j)
                before += n_rel[direction]

        def general_sync(sp):
            sp.wait_ge(general_known, 1)
            found = sp.value_load(general[0:1, 0:1], min_val=0, max_val=1)
            for k in range(2):
                sp.wait_ge(stored[k], 16 * (n_groups // 2 + k))
            with sp.If(found > 0):
                sp.dma_start(g_a[:], a_all).then_inc(g_a_loaded, 16)
                for direction, of in enumerate(biases):
                    sp.dma_start(g_bias[direction][:], of.rearrange("(a r) d -> a r d", a=1)
                                 .broadcast_to([P, n_rel[direction], 2 * P])).then_inc(g_bias_loaded, 16)
                with sp.Fori(0, n_graphs) as b:
                    sp.dma_start(g_x[:], x[b]).then_inc(g_loaded, 16)
                    sp.dma_start(g_adj[:], adj[b]).then_inc(g_loaded, 16)

                    sp.wait_ge(g_out_ready, b + 1)
                    sp.dma_start(out[b], g_out[:]).then_inc(g_stored, 16)
                    wait_alone(nc.sync, g_stored, 16 * (b + 1))
            sp.nop()

        def general_pool(pool):
            pool.wait_ge(general_known, 1)
            found = pool.value_load(general[0:1, 0:1], min_val=0, max_val=1)
            with pool.If(found > 0):
                with pool.Fori(0, 2 * n_graphs) as n:
                    wait_alone(nc.gpsimd, g_mv_ready, n + 1)
                    nc.gpsimd.tensor_scalar(g_var[:], g_mv[:, 1:2], EPS, None, ALU.add).then_inc(g_var_ready, 1)
                    pool.wait_ge(g_var_ready, n + 1)
                    nc.gpsimd.tensor_tensor(g_rstd[:], g_var[:], minus_half[:, 0:1], ALU.pow)\
                        .then_inc(g_rstd_ready, 1)
            pool.nop()

        def general_scalar(act):
            act.wait_ge(general_known, 1)
            found = act.value_load(general[0:1, 0:1], min_val=0, max_val=1)
            with act.If(found > 0):
                with act.Fori(0, n_graphs) as b:
                    act.wait_ge(g_score_ready, b + 1)
                    nc.scalar.activation(g_prob[:], g_score[:], ACT.Exp, bias=g_nmax[:], accum_out=g_z[:])\
                        .then_inc(g_prob_ready, 1)

                    def tanh_of_gate(n, direction, j):
                        act.wait_ge(g_gate_in, 3 * (n + 1))
                        nc.scalar.activation(g_tanh[:], g_g[:], ACT.Tanh, scale=0.5).then_inc(g_tanh_ready, 1)

                    each_term(act, b, tanh_of_gate)
            act.nop()

        def general_vector(dve):
            dve.wait_ge(general_known, 1)
            found = dve.value_load(general[0:1, 0:1], min_val=0, max_val=1)
            with dve.If(found > 0):
                dve.wait_ge(g_w_made, 6)
                nc.vector.tensor_copy(g_w[:, LOOP], p_hg[:, 0]).then_inc(g_w_ready, 1)
                nc.vector.tensor_copy(g_w[:, FWD], p_hg[:, 1]).then_inc(g_w_ready, 1)
                nc.vector.tensor_copy(g_w[:, BWD], p_hg[:, 2]).then_inc(g_w_ready, 1)
                dve.wait_ge(g_a_loaded, 16)
                dve.wait_ge(g_bias_loaded, 16 * 3)

                with dve.Fori(0, n_graphs) as b:
                    def stats(n):
                        dve.wait_ge(g_res_ready, n)
                        nc.vector.bn_stats(g_stats[:], g_res[:]).then_inc(g_stats_ready, 1)
                        wait_alone(nc.vector, g_stats_ready, n)
                        nc.vector.bn_aggr(g_mv[:], g_stats[:]).then_inc(g_mv_ready, 1)
                        dve.wait_ge(g_rstd_ready, n)

                    dve.wait_ge(g_loaded, 32 * (b + 1))
                    nc.vector.tensor_copy(g_adjf[:, 0], g_adj[:]).then_inc(g_adjf_ready, 1)
                    dve.wait_ge(g_turned, 2 * (b + 1))
                    nc.vector.tensor_copy(g_xt[:], p_e[:, 1, 0]).then_inc(g_xt_ready, 1)
                    nc.vector.tensor_copy(g_adjf[:, 1], p_e[:, 1, 1]).then_inc(g_xt_ready, 1)
                    dve.wait_ge(g_xt_ready, 2 * (b + 1))
                    for k in range(KINDS):
                        nc.vector.tensor_scalar(g_xa[:, k], g_xt[:], g_a[:, k:k + 1], None, ALU.mult)\
                            .then_inc(g_xa_ready, 1)
                    dve.wait_ge(g_e_made, b + 1)
                    nc.vector.tensor_scalar(g_fifth[:], p_e[:, 0], SLOPE, None, ALU.mult).then_inc(g_attn, 1)
                    own = 2 + 2 * KINDS + 1
                    dve.wait_ge(g_attn, own * b + 1)
                    nc.vector.tensor_tensor(g_leaky[:], p_e[:, 0], g_fifth[:], ALU.max).then_inc(g_attn, 1)
                    for k in range(KINDS):
                        nc.vector.tensor_scalar(g_is[:, k], g_adjf[:, 0], float(k + 1), None, ALU.is_equal)\
                            .then_inc(g_attn, 1)
                    nc.vector.memset(g_score[:], NEG_INF).then_inc(g_attn, 1)
                    for k in range(KINDS):
                        wait_alone(nc.vector, g_attn, own * b + 3 + KINDS + k)
                        nc.vector.copy_predicated(g_score[:], g_is[:, k], g_leaky[:, k]).then_inc(g_attn, 1)
                    dve.wait_ge(g_attn, own * (b + 1))
                    nc.vector.tensor_reduce(g_nmax[:], g_score[:], AX_X, ALU.max, negate=True)\
                        .then_inc(g_score_ready, 1)
                    dve.wait_ge(g_prob_turned, b + 1)
                    nc.vector.tensor_copy(g_prob_t[:], p_ut[:, 0]).then_inc(g_prob_t_ready, 1)
                    nc.vector.reciprocal(g_rz[:], g_z[:]).then_inc(g_rz_ready, 1)
                    dve.wait_ge(g_rz_ready, b + 1)
                    dve.wait_ge(g_attended, b + 1)
                    nc.vector.scalar_tensor_tensor(out=g_res[:], in0=p_o[:, 0], scalar=g_rz[:], in1=g_x[:],
                                                   op0=ALU.mult, op1=ALU.add).then_inc(g_res_ready, 1)
                    stats(2 * b + 1)
                    nc.vector.tensor_scalar(g_y[:], g_res[:], g_mv[:, 0:1], g_rstd[:], ALU.subtract, ALU.mult)\
                        .then_inc(g_y_ready, 1)
                    dve.wait_ge(g_y_turned, b + 1)
                    nc.vector.tensor_copy(g_y_t[:], p_yt[:, 0]).then_inc(g_y_t_ready, 1)
                    dve.wait_ge(g_hg_made, b + 1)
                    nc.vector.tensor_copy(g_hg[:], p_hg[:, 0:3]).then_inc(g_hg_ready, 1)
                    nc.vector.memset(g_acc[:], 0.0).then_inc(g_hg_ready, 1)
                    dve.wait_ge(g_hg_ready, 2 * (b + 1))

                    def set_relation(b, direction):
                        nc.vector.memset(g_rel[:], float(first_rel[direction])).then_inc(g_rel_set, 1)

                    def term(n, direction, j):
                        dve.wait_ge(g_rel_set, n + b * 3 + direction + 1)
                        nc.vector.tensor_scalar(g_sel[:], g_adjf[:, 1 if direction == FWD else 0], g_rel[:], 0.5,
                                                ALU.is_equal, ALU.mult).then_inc(g_gate_in, 1)
                        bias = g_bias[direction][:, bass.ds(j, 1)].rearrange("p a n -> p (a n)")
                        nc.vector.tensor_tensor(g_h[:], g_hg[:, direction, 0], bias[:, 0:P], ALU.add)\
                            .then_inc(g_gate_in, 1)
                        nc.vector.tensor_tensor(g_g[:], g_hg[:, direction, 1], bias[:, P:2 * P], ALU.add)\
                            .then_inc(g_gate_in, 1)
                        dve.wait_ge(g_gate_in, 3 * (n + 1))
                        nc.vector.tensor_scalar(g_rel[:], g_rel[:], 1.0, None, ALU.add).then_inc(g_rel_set, 1)
                        dve.wait_ge(g_tanh_ready, n + 1)
                        nc.vector.scalar_tensor_tensor(out=g_vals[:], in0=g_tanh[:], scalar=1.0, in1=g_h[:],
                                                       op0=ALU.add, op1=ALU.mult).then_inc(g_vals_ready, 1)
                        dve.wait_ge(g_term_made, n + 1)
                        nc.vector.tensor_tensor(g_acc[:], p_ag[:, 0], g_acc[:], ALU.add).then_inc(g_term_added, 1)
                        dve.wait_ge(g_rel_set, n + b * 3 + direction + 2)
                        dve.wait_ge(g_term_added, n + 1)

                    each_term(dve, b, term, set_relation)
                    dve.wait_ge(g_term_added, terms * (b + 1))
                    nc.vector.scalar_tensor_tensor(out=g_res[:], in0=g_acc[:], scalar=0.0, in1=g_y[:],
                                                   op0=ALU.max, op1=ALU.add).then_inc(g_res_ready, 1)
                    stats(2 * b + 2)
                    nc.vector.tensor_scalar(g_out[:], g_res[:], g_mv[:, 0:1], g_rstd[:], ALU.subtract, ALU.mult)\
                        .then_inc(g_out_ready, 1)
            dve.nop()

        def general_tensor(pe):
            pe.wait_ge(general_known, 1)
            found = pe.value_load(general[0:1, 0:1], min_val=0, max_val=1)
            with pe.If(found > 0):
                pe.wait_ge(mv2_done, G * n_groups)
                for k in range(3):
                    nc.tensor.transpose(p_hg[:, k, 0], w_rows[:, k], ident[:]).then_inc(g_w_made, 1)
                    nc.tensor.matmul(p_hg[:, k, 1], w_rows[:, k], wg_s[:, k], start=True, stop=True)\
                        .then_inc(g_w_made, 1)
                pe.wait_ge(g_w_ready, 3)

                with pe.Fori(0, n_graphs) as b:
                    pe.wait_ge(g_loaded, 32 * (b + 1))
                    nc.tensor.transpose(p_e[:, 1, 0], g_x[:], ident[:]).then_inc(g_turned, 1)
                    pe.wait_ge(g_adjf_ready, b + 1)
                    nc.tensor.transpose(p_e[:, 1, 1], g_adjf[:, 0], ident[:]).then_inc(g_turned, 1)
                    pe.wait_ge(g_xa_ready, KINDS * (b + 1))
                    for k in range(KINDS):
                        last = nc.tensor.matmul(p_e[:, 0, k], g_xa[:, k], g_xt[:], start=True, stop=True)
                    last.then_inc(g_e_made, 1)
                    pe.wait_ge(g_prob_ready, b + 1)
                    nc.tensor.transpose(p_ut[:, 0], g_prob[:], ident[:]).then_inc(g_prob_turned, 1)
                    pe.wait_ge(g_prob_t_ready, b + 1)
                    nc.tensor.matmul(p_o[:, 0], g_prob_t[:], g_x[:], start=True, stop=True).then_inc(g_attended, 1)
                    pe.wait_ge(g_y_ready, b + 1)
                    nc.tensor.transpose(p_yt[:, 0], g_y[:], ident[:]).then_inc(g_y_turned, 1)
                    pe.wait_ge(g_y_t_ready, b + 1)
                    for k in range(3):
                        last = nc.tensor.matmul(p_hg[:, k], g_y_t[:], g_w[:, k], start=True, stop=True)
                    last.then_inc(g_hg_made, 1)

                    def sum_of_relation(n, direction, j):
                        pe.wait_ge(g_vals_ready, n + 1)
                        nc.tensor.matmul(p_ag[:, 0], g_sel[:], g_vals[:], start=True, stop=True)\
                            .then_inc(g_term_made, 1)

                    each_term(pe, b, sum_of_relation)
            pe.nop()

        block = ctx.enter_context(nc.Block())

        def wait_alone(eng, semaphore, value):
            eng.wait_ge(semaphore, value)
            eng.sem_inc(wait_over[eng], 1)

        def half(h):
            return slice(h * G // 2, (h + 1) * G // 2)

        def is_first(g, n=1):
            return isinstance(g, int) and g < n

        def is_late(g):
            return isinstance(g, int) and g >= n_groups - LATE

        def of_half(f, h):
            return lambda g, s: f(g, s, h)

        engines = {"tensor": nc.tensor, "scalar": nc.scalar, "vector": nc.vector, "gpsimd": nc.gpsimd}

        def run(eng, stages):
            turns, head, body, tail = SCHEDULE[eng]

            def do(name, turn=None):
                stage, group = name.split(":")
                g, f = int(group), stages[stage]
                if turn is None:
                    f(g, g % UNROLL)
                else:
                    f(turn * UNROLL + g, g % UNROLL)

            order = head.split(), body.split(), tail.split()
            names = [n.split(":")[0] for n in order[1]]
            assert sorted(names) == sorted(set(stages) - {"finish"})
            done = list(order[0])
            for name in order[0]:
                do(name)
            with engines[eng].Fori(0, turns) as turn:
                for u in range(UNROLL):
                    for name in order[1]:
                        stage, k = name.split(":")
                        do(f"{stage}:{int(k) + u}", turn)
                        done += [f"{stage}:{int(k) + u + UNROLL * i}" for i in range(turns)]
            for name in order[2]:
                do(name)
            done += order[2]
            done = [name for name in done if not name.startswith("finish:")]
            assert sorted(done) == sorted(f"{x}:{g}" for x in names for g in range(n_groups))

        def nth(g, s, slots, per=1):
            return (g - s) // slots + 1

        @block.sync
        def _(sp):
            def load(g, s):
                sp.dma_start(xt[:, s], x_t_v[g]).then_inc(xt_loaded[s], 16)
                sp.dma_start(adj_s[:, s], adj_v[g]).then_inc(adj_loaded[s], 16)
                sp.dma_start(x_s[:, s], x_v[g]).then_inc(x_loaded[s], 16)

            load(0, 0)
            sp.dma_start(w_rows[:], w.rearrange("k f d -> f k d")).then_inc(w_loaded, 16)
            sp.dma_start(wg_s[:], wg_t.rearrange("k f e -> f k e")).then_inc(w_loaded, 16)
            for g in range(1, 4):
                load(g, g)

            def store(g, s):
                if is_late(g):
                    for h in range(2):
                        sp.wait_ge(finish_done, G * (g - n_groups + LATE) + 2 * h + 2)
                        if g == n_groups - 1:
                            sp.dma_start(out_v[g, :, 2 * h:2 * h + 2], out_s[:, s % 2, half(h)]).then_inc(stored[s % 2], 16)
                    if g < n_groups - 1:
                        sp.dma_start(out_v[g], out_s[:, s % 2]).then_inc(stored[s % 2], 16)
                    return
                sp.wait_ge(out_done, g + 1)
                sp.dma_start(out_v[g], out_s[:, s % 2]).then_inc(stored[s % 2], 16)

            def reload(g, s):
                sp.wait_ge(r1_done, G * (g + 1))
                sp.wait_ge(mask_done, g + 1)
                sp.wait_ge(absent_done, g + 1)
                load(g + UNROLL, s)

            reload(0, 0)
            with sp.Fori(0, n_groups // UNROLL - 2) as turn:
                for s in range(1, UNROLL + 1):
                    g = turn * UNROLL + s
                    reload(g, s % UNROLL)
                    store(g - 1, (s - 1) % UNROLL)
            for g in range(n_groups - 2 * UNROLL + 1, n_groups - UNROLL):
                reload(g, g % UNROLL)
                store(g - 1, (g - 1) % UNROLL)
            for g in range(n_groups - UNROLL - 1, n_groups):
                store(g, g % UNROLL)
            general_sync(sp)

        @block.gpsimd
        def _(pool):
            nc.gpsimd.memset(ident[:], 0.0).then_inc(const_done, 1)
            nc.gpsimd.memset(penalties[:], 0.0).then_inc(const_done, 1)
            nc.gpsimd.memset(ones3[:], 1.0).then_inc(const_done, 1)
            nc.gpsimd.memset(ones_col[:], 1.0).then_inc(const_done, 1)
            nc.gpsimd.memset(minus_one[:], -1.0).then_inc(const_done, 1)
            nc.gpsimd.memset(minus_half[:], -0.5).then_inc(cent_done, 1)
            pool.wait_ge(const_done, 2)
            for m, fill in ((ident, 1.0), (penalties, -PENALTY)):
                nc.gpsimd.affine_select(out=m[:], in_=m[:], compare_op=ALU.not_equal, fill=fill, base=0,
                                        pattern=[[-1, P]], channel_multiplier=1).then_inc(ident_done, 1)
            pool.wait_ge(const_done, 5)
            pool.wait_ge(cent_done, 1)

            def norm1(g, s):
                k = s % 2
                wait_alone(nc.gpsimd, mv1_done, G * (g + 1))
                nc.gpsimd.tensor_scalar(rs1[:, k, 0], mv1[:, s, :, 1], EPS, None, ALU.add).then_inc(pool1, 1)
                pool.wait_ge(pool1, 2 * g + 1)
                nc.gpsimd.tensor_tensor(rs1[:, k, 1], rs1[:, k, 0], minus_half[:], ALU.pow).then_inc(pool1, 1)
                pool.wait_ge(pool1, 2 * g + 2)
                nc.gpsimd.tensor_tensor(y[:, s], res1[:, k], rs1[:, k, 1, :, None].broadcast_to([P, G, P]),
                                        ALU.mult).then_inc(y_done, 1)

            def norm2(g, s):
                k = s % 2
                wait_alone(nc.gpsimd, mv2_done, G * (g + 1))
                nc.gpsimd.tensor_scalar(rs2[:, s, 0], mv2[:, s, :, 1], EPS, None, ALU.add).then_inc(pool2, 1)
                if is_late(g):
                    nc.gpsimd.tensor_tensor(shift[:, s, 0], mv2[:, s, :, 0], minus_one[:], ALU.mult).then_inc(shift_done, 1)
                    pool.wait_ge(pool2, 2 * g + 1)
                    nc.gpsimd.tensor_tensor(rs2[:, s, 1], rs2[:, s, 0], minus_half[:], ALU.pow).then_inc(pool2, 1)
                    pool.wait_ge(pool2, 2 * g + 2)
                    pool.wait_ge(shift_done, 2 * (g - n_groups + LATE) + 1)
                    nc.gpsimd.tensor_tensor(shift[:, s, 1], shift[:, s, 0], rs2[:, s, 1], ALU.mult).then_inc(shift_done, 1)
                    return
                if not is_first(g):
                    pool.wait_ge(out_done, g)
                nc.gpsimd.tensor_tensor(cent[:], res2[:, k], mv2[:, s, :, 0:1].broadcast_to([P, G, P]),
                                        ALU.subtract).then_inc(cent_done, 1)
                pool.wait_ge(pool2, 2 * g + 1)
                nc.gpsimd.tensor_tensor(rs2[:, s, 1], rs2[:, s, 0], minus_half[:], ALU.pow).then_inc(pool2, 1)
                pool.wait_ge(pool2, 2 * g + 2)
                pool.wait_ge(cent_done, g + 2)
                if not is_first(g, 2):
                    pool.wait_ge(stored[k], 16 * ((g - k) // 2))
                nc.gpsimd.tensor_tensor(out_s[:, k], cent[:], rs2[:, s, 1, :, None].broadcast_to([P, G, P]),
                                        ALU.mult).then_inc(out_done, 1)

            run("gpsimd", {"norm1": norm1, "norm2": norm2})
            general_pool(pool)

        @block.scalar
        def _(act):
            def absents(g, s):
                act.wait_ge(adj_loaded[s], 16 * nth(g, s, 4))
                nc.scalar.activation(absent[:, s % 2], adj_s[:, s], ACT.Relu, scale=-1.0, bias=1.0,
                                     accum_out=sums[:, 0, bass.ds(g, 1)]).then_inc(absent_done, 1)

            def masks(g, s):
                act.wait_ge(adj_loaded[s], 16 * nth(g, s, 4))
                nc.scalar.activation(mask[:, s], adj_s[:, s], ACT.Relu,
                                     accum_out=sums[:, 1, bass.ds(g, 1)]).then_inc(mask_done, 1)

            def weigh(g, s):
                if is_first(g):
                    act.wait_ge(a_loaded, 16)
                act.wait_ge(xt_loaded[s], 16 * nth(g, s, 4))
                nc.scalar.activation(xat[:, s % 2], xt[:, s], ACT.Copy, scale=a_col[:]).then_inc(xat_done, 1)

            def rel(g, s):
                act.wait_ge(e_done, g + 1)
                nc.scalar.activation(rel4[:, s % 2], p_e[:, s % 2], ACT.Relu,
                                     scale=1.0 / SLOPE - 1.0).then_inc(rel4_done, 1)

            def exps(g, s):
                k = s % 2
                for i in range(G):
                    act.wait_ge(score_done, G * g + i + 1)
                    nc.scalar.activation(prob[:, k, i], nscore[:, k, i], ACT.Exp, scale=-1.0,
                                         bias=nmax[:, s, i:i + 1],
                                         accum_out=psumz[:, s, i:i + 1]).then_inc(exp_done, 1)

            def evac_ut(g, s):
                if is_first(g):
                    act.wait_ge(w_pe, 2)
                    nc.scalar.activation(w_both[:, 0:P], p_hg[:, 0, 0], ACT.Copy, scale=0.5).then_inc(w_ready, 1)
                    nc.scalar.activation(w_both[:, P:2 * P], p_hg[:, 0, 1], ACT.Copy).then_inc(w_ready, 1)
                act.wait_ge(tu_done, g + 1)
                nc.scalar.activation(prob_t[:, s % 2], p_ut[:], ACT.Copy).then_inc(ut_done, 1)

            def evac_yt(g, s):
                act.wait_ge(ty_done, g + 1)
                nc.scalar.activation(y_t[:, s % 2], p_yt[:], ACT.Copy).then_inc(yt_done, 1)

            def tanh(g, s, h):
                act.wait_ge(hg_done[h], g + 1)
                nc.scalar.activation(th[:, s % 2, half(h)], p_hg[:, half(h), 1], ACT.Tanh, scale=0.5)\
                    .then_inc(tanh_done[h], 1)

            def finish(g, s):
                k = s % 2
                act.wait_ge(shift_done, 2 * (g - n_groups + LATE) + 2)
                act.wait_ge(pool2, 2 * g + 2)
                act.wait_ge(r2_done, g + 1)
                act.wait_ge(stored[k], 16 * (g // 2))
                for i in range(G):
                    nc.scalar.activation(out_s[:, k, i], res2[:, k, i], ACT.Identity, scale=rs2[:, s, 1, i:i + 1],
                                         bias=shift[:, s, 1, i:i + 1]).then_inc(finish_done, 1)

            nc.scalar.dma_start(a_col[:], a_0).then_inc(a_loaded, 16)
            nc.scalar.dma_start(b_rows[:], b_loop.broadcast_to([3, 2 * P])).then_inc(b_loaded, 16)
            act.wait_ge(cent_done, 1)
            nc.scalar.activation(table_loader[:], minus_half[:, 0:1], ACT.Exp).then_inc(table_loaded, 1)
            run("scalar", {"weigh": weigh, "turned_probs": evac_ut, "absent": absents, "mask": masks, "relu": rel,
                           "turned_y": evac_yt, "exp": exps, "tanh_a": of_half(tanh, 0), "tanh_b": of_half(tanh, 1), "finish": finish})
            general_scalar(act)

        @block.vector
        def _(dve):
            nc.vector.memset(warm[:], 0.0).then_inc(warm_ready, 1)
            dve.wait_ge(b_loaded, 16)
            nc.vector.tensor_scalar(b_rest[:, 0, 0:P], b_rows[:, 0:P], 0.5, None, ALU.mult).then_inc(b_step, 1)
            nc.vector.tensor_copy(b_rest[:, 0, P:2 * P], b_rows[:, P:2 * P]).then_inc(b_step, 1)
            dve.wait_ge(b_step, 2)
            nc.vector.tensor_copy(b_part[:, 0], b_rest[:, 0]).then_inc(b_step, 1)
            dve.wait_ge(b_step, 3)
            nc.vector.tensor_tensor(b_rest[:, 1], b_rest[:, 0], b_part[:, 0], ALU.subtract).then_inc(b_step, 1)
            dve.wait_ge(b_step, 4)
            nc.vector.tensor_copy(b_part[:, 1], b_rest[:, 1]).then_inc(b_step, 1)
            dve.wait_ge(b_step, 5)
            nc.vector.tensor_tensor(b_part[:, 2], b_rest[:, 1], b_part[:, 1], ALU.subtract).then_inc(b_step, 1)
            dve.wait_ge(w_loaded, 16 * 2)
            nc.vector.bn_stats(w_stats[:], w_rows[:, LOOP]).then_inc(w_step, 1)
            dve.wait_ge(w_step, 1)
            nc.vector.bn_aggr(w_mean[:], w_stats[:]).then_inc(w_step, 1)
            dve.wait_ge(w_step, 2)
            nc.vector.tensor_scalar(w_mid[:], w_rows[:, LOOP], w_mean[:, 0:1], None, ALU.subtract).then_inc(w_step, 1)

            def place_biases():
                dve.wait_ge(ident_done, 1)
                nc.vector.tensor_scalar(b_sum[:, 0], b_part[:, 0], ident[0:3, 0:1], None, ALU.mult).then_inc(b_step, 1)
                dve.wait_ge(b_step, 7)
                nc.vector.scalar_tensor_tensor(out=b_sum[:, 1], in0=b_part[:, 1], scalar=ident[0:3, 1:2],
                                               in1=b_sum[:, 0], op0=ALU.mult, op1=ALU.add).then_inc(b_step, 1)
                dve.wait_ge(b_step, 8)
                for k in range(2):
                    nc.vector.scalar_tensor_tensor(out=b_parts[:, k], in0=b_part[:, 2], scalar=ident[0:3, 2:3],
                                                   in1=b_sum[:, 1], op0=ALU.mult, op1=ALU.add).then_inc(b_step, 1)

            def scores(g, s):
                k = s % 2
                wait_alone(nc.vector, rel4_done, g + 1)
                for i in range(G):
                    nc.vector.tensor_tensor_reduce(nscore[:, k, i], p_e[:, k, i], rel4[:, k, i], -SLOPE, FLOAT_MAX,
                                                   ALU.add, ALU.min, nmax[:, s, i:i + 1]).then_inc(score_done, 1)

            def invert(g, s):
                if is_first(g):
                    place_biases()
                dve.wait_ge(exp_done, G * (g + 1))
                nc.vector.reciprocal(rz[:, s], psumz[:, s]).then_inc(rz_done, 1)

            def residual1(g, s):
                k = s % 2
                dve.wait_ge(rz_done, g + 1)
                dve.wait_ge(av_done, g + 1)
                if not is_first(g, 2):
                    dve.wait_ge(y_done, g - 1)
                for i in range(G):
                    nc.vector.scalar_tensor_tensor(out=res1[:, k, i], in0=p_o[:, i], scalar=rz[:, s, i:i + 1],
                                                   in1=x_s[:, s, i], op0=ALU.mult, op1=ALU.add).then_inc(r1_done, 1)

            def stats1(g, s):
                k = s % 2
                for i in range(G):
                    dve.wait_ge(r1_done, G * g + i + 1)
                    nc.vector.bn_stats(st1[:, s, i], res1[:, k, i]).then_inc(st1_done, 1)

            def means1(g, s):
                wait_alone(nc.vector, st1_done, G * (g + 1))
                for i in range(G):
                    nc.vector.bn_aggr(mv1[:, s, i], st1[:, s, i]).then_inc(mv1_done, 1)

            def values(g, s, h):
                k = s % 2
                dve.wait_ge(tanh_done[h], g + 1)
                nc.vector.scalar_tensor_tensor(out=vals[:, k, half(h)], in0=th[:, k, half(h)], scalar=1.0,
                                               in1=p_hg[:, half(h), 0], op0=ALU.add, op1=ALU.mult)\
                    .then_inc(vals_done[h], 1)

            def residual2(g, s):
                k = s % 2
                dve.wait_ge(ag_done[0], g + 1)
                dve.wait_ge(ag_done[1], g + 1)
                if not is_first(g, 2) and not is_late(g - 2):
                    dve.wait_ge(cent_done, g)
                if is_late(g) and is_late(g - 2):
                    dve.wait_ge(finish_done, G * (g - 1 - n_groups + LATE))
                nc.vector.scalar_tensor_tensor(out=res2[:, k], in0=p_ag[:], scalar=0.0, in1=y[:, s],
                                               op0=ALU.max, op1=ALU.add).then_inc(r2_done, 1)

            def stats2(g, s):
                k = s % 2
                dve.wait_ge(r2_done, g + 1)
                for i in range(G):
                    nc.vector.bn_stats(st2[:, s, i], res2[:, k, i]).then_inc(st2_done, 1)

            def means2(g, s):
                wait_alone(nc.vector, st2_done, G * (g + 1))
                for i in range(G):
                    nc.vector.bn_aggr(mv2[:, s, i], st2[:, s, i]).then_inc(mv2_done, 1)

            run("vector", {"scores": scores, "inverse": invert, "residual1": residual1, "stats1": stats1, "means1": means1,
                           "values_a": of_half(values, 0), "values_b": of_half(values, 1),
                           "residual2": residual2, "stats2": stats2, "means2": means2})

            dve.wait_ge(mask_done, n_groups)
            nc.vector.tensor_reduce(sum_rows[:], sums[:], AX_XY, ALU.add).then_inc(sum_done, 1)
            dve.wait_ge(sum_done, 2)
            nc.vector.tensor_scalar(general[:], p_e[0:1, 0, 0, 0:1], float(x.shape[0] * P * P), None,
                                    ALU.is_gt).then_inc(general_known, 1)
            general_vector(dve)

        @block.tensor
        def _(pe):
            pe.wait_ge(warm_ready, 1)
            for i in range(10):
                nc.tensor.matmul(p_ag[:, 0], warm[:], warm[:], start=True, stop=True).then_inc(warmed, 1)
            pe.wait_ge(ident_done, 2)

            def score(g, s):
                k = s % 2
                if not is_first(g, 2):
                    pe.wait_ge(score_done, G * (g - 1))
                pe.wait_ge(absent_done, g + 1)
                nc.tensor.matmul(p_e[:, k], penalties[:], absent[:, k], start=True, stop=False, skip_group_check=True)
                pe.wait_ge(xt_loaded[s], 16 * nth(g, s, 4))
                pe.wait_ge(xat_done, g + 1)
                for i in range(G):
                    last = nc.tensor.matmul(p_e[:, k, i], xat[:, k, i], xt[:, s, i], start=False, stop=(i == G - 1),
                                            skip_group_check=True)
                last.then_inc(e_done, 1)

            def transpose_u(g, s):
                if not is_first(g):
                    pe.wait_ge(ut_done, g)
                k = s % 2
                if is_first(g):
                    pe.wait_ge(w_step, 3)
                    nc.tensor.transpose(p_hg[:, 0, 0], w_mid[:], ident[:]).then_inc(w_pe, 1)
                    nc.tensor.matmul(p_hg[:, 0, 1], w_mid[:], wg_s[:, LOOP], start=True, stop=True)\
                        .then_inc(w_pe, 1)
                for i in range(G):
                    pe.wait_ge(exp_done, G * g + i + 1)
                    last = nc.tensor.transpose(p_ut[:, i], prob[:, k, i], ident[:])
                last.then_inc(tu_done, 1)

            def attend(g, s):
                k = s % 2
                pe.wait_ge(ut_done, g + 1)
                pe.wait_ge(x_loaded[s], 16 * nth(g, s, 4))
                if not is_first(g):
                    pe.wait_ge(r1_done, G * g)
                for i in range(G):
                    last = nc.tensor.matmul(p_o[:, i], prob_t[:, k, i], x_s[:, s, i], start=True, stop=True)
                last.then_inc(av_done, 1)

            def transpose_y(g, s):
                if not is_first(g):
                    pe.wait_ge(yt_done, g)
                k = s % 2
                pe.wait_ge(y_done, g + 1)
                for i in range(G):
                    last = nc.tensor.transpose(p_yt[:, i], y[:, s, i], ident[:])
                last.then_inc(ty_done, 1)

            def gate(g, s, h):
                if not is_first(g):
                    pe.wait_ge(vals_done[h], g)
                k = s % 2
                if is_first(g):
                    pe.wait_ge(w_ready, 2)
                    pe.wait_ge(b_step, 10)
                pe.wait_ge(yt_done, g + 1)
                nc.tensor.matmul(p_hg[:, half(h)], ones3[:], b_parts[:], start=True, stop=False,
                                 skip_group_check=True)
                for i in range(2 * h, 2 * h + 2):
                    last = nc.tensor.matmul(p_hg[:, i], y_t[:, k, i], w_both[:], start=False, stop=(i % 2 == 1),
                                            skip_group_check=True)
                last.then_inc(hg_done[h], 1)

            def neighbours(g, s, h):
                if not is_first(g):
                    pe.wait_ge(r2_done, g)
                k = s % 2
                pe.wait_ge(vals_done[h], g + 1)
                pe.wait_ge(mask_done, g + 1)
                for i in range(2 * h, 2 * h + 2):
                    last = nc.tensor.matmul(p_ag[:, i], mask[:, s, i], vals[:, k, i], start=True, stop=True)
                last.then_inc(ag_done[h], 1)

            run("tensor", {"turn_probs": transpose_u, "turn_y": transpose_y,
                           "products": score, "attend": attend,
                           "gate_a": of_half(gate, 0), "gate_b": of_half(gate, 1),
                           "sum_a": of_half(neighbours, 0), "sum_b": of_half(neighbours, 1)})

            pe.wait_ge(sum_done, 1)
            nc.tensor.matmul(p_e[0:1, 0, 0, 0:1], sum_rows[:], ones_col[:], start=True, stop=True)\
                .then_inc(sum_done, 1)
            general_tensor(pe)


def kernel(x, adj, nodemask, L0_gnn_a_0, L0_gnn_a_1, L0_gnn_a_2, L0_gnn_a_3,
           L1_gnn_W_fwd, L1_gnn_W_bwd, L1_gnn_W_loop, L1_gnn_Wg_fwd, L1_gnn_Wg_bwd, L1_gnn_Wg_loop,
           L1_gnn_b_fwd, L1_gnn_b_bwd, L1_gnn_b_loop, L1_gnn_bg_fwd, L1_gnn_bg_bwd, L1_gnn_bg_loop):
    import numpy as np
    import concourse.bacc as bacc
    from concourse.bass_utils import run_bass_kernel_spmd

    def turned(a):
        return np.asarray(a).T

    def b_and_bg(b, bg):
        return np.concatenate([b, bg], axis=1)

    arrays = {
        "x": x, "x_t": np.swapaxes(np.asarray(x), 1, 2), "adj": adj, "a_0": L0_gnn_a_0,
        "a_all": np.concatenate([L0_gnn_a_0, L0_gnn_a_1, L0_gnn_a_2, L0_gnn_a_3], axis=1),
        "w": np.stack([L1_gnn_W_loop, L1_gnn_W_fwd, L1_gnn_W_bwd]),
        "wg_t": np.stack([turned(L1_gnn_Wg_loop), turned(L1_gnn_Wg_fwd), turned(L1_gnn_Wg_bwd)]),
        "b_loop": b_and_bg(L1_gnn_b_loop, L1_gnn_bg_loop),
        "b_fwd": b_and_bg(L1_gnn_b_fwd, L1_gnn_bg_fwd), "b_bwd": b_and_bg(L1_gnn_b_bwd, L1_gnn_bg_bwd),
    }
    arrays = {name: np.ascontiguousarray(a) for name, a in arrays.items()}
    nc = bacc.Bacc("TRN2", target_bir_lowering=False, num_devices=1)
    aps = {name: nc.dram_tensor(name, a.shape, mybir.dt.from_np(a.dtype), kind="ExternalInput").ap()
           for name, a in arrays.items()}
    out = nc.dram_tensor("out", arrays["x"].shape, F32, kind="ExternalOutput").ap()
    program(nc, **aps, out=out)
    r = run_bass_kernel_spmd(nc, [arrays], core_ids=[0])
    return r.results[0]["out"]
```
